# Optimizing a Trainium2 kernel written in Bass

```python
import numpy as np
import jax
import jax.numpy as jnp

def _softmax(x, axis=-1):
    return jax.nn.softmax(x, axis=axis)

def _gelu(x):
    return jax.nn.gelu(x, approximate=True)

def _silu(x):
    return jax.nn.silu(x)

def _sigmoid(x):
    return jax.nn.sigmoid(x)

def _layernorm(x, axis=-1, eps=1e-05):
    m = jnp.mean(x, axis=axis, keepdims=True)
    v = jnp.var(x, axis=axis, keepdims=True)
    return (x - m) / jnp.sqrt(v + eps)

def _scatter_add(tgt, idx, src, axis=0):
    return tgt.at[idx].add(src)

def _segment_sum(src, seg, n):
    return jax.ops.segment_sum(src, seg, n)
kernel_name = 'mk_decoder_preln_d1_seqx_r2_4d5424'

def setup_inputs(seed: int=0):
    np.random.seed(seed)
    _w = jnp.asarray

    def _rec_inputs():
        import jax
        import jax.numpy as jnp
        _rk = jax.random.key(seed)
        x = 7.22e-05 + 1 * jax.random.normal(jax.random.fold_in(_rk, 1), (4, 1024, 512), jnp.float32)
        _lenS = 1024 - jax.random.randint(jax.random.fold_in(_rk, 7), (4,), 0, max(1, 1024 // 4) + 1, jnp.int32)
        _lenS2 = 64 - jax.random.randint(jax.random.fold_in(_rk, 8), (4,), 0, max(1, 64 // 4) + 1, jnp.int32)
        _ctx_1024P = jax.random.normal(jax.random.fold_in(_rk, 11), (4, 16, 512), jnp.float32)
        _ctx_1024c = jax.random.dirichlet(jax.random.fold_in(_rk, 511), 0.3 * jnp.ones((16,), jnp.float32), (4, 64))
        _ctx_1024t = jnp.einsum('bsk,bkd->bsd', _ctx_1024c, _ctx_1024P)
        _ctx_1024t = _ctx_1024t * jax.lax.rsqrt(jnp.mean(jnp.square(_ctx_1024t)) + 1e-12) * 0.953939
        ctx_1024 = 2.81802e-05 + 1.00001 * (_ctx_1024t + 0.3 * jax.random.normal(jax.random.fold_in(_rk, 611), (4, 64, 512), jnp.float32))
        return (x, ctx_1024)
    x, ctx_1024 = _rec_inputs()

    def _L0_attn_setup():
        import jax, jax.numpy as jnp
        import numpy as np
        NUM_HEADS = 16
        HEAD_DIM = 64
        NEG_INF = -1000000000.0

        def rotary_embedding(x, seq_len, head_dim):
            positions = jnp.arange(seq_len)
            dim_pairs = jnp.arange(0, head_dim, 2)
            freqs = 1.0 / 10000.0 ** (dim_pairs / head_dim)
            angles = positions[:, None] * freqs[None, :]
            cos = jnp.cos(angles)[:, None, :]
            sin = jnp.sin(angles)[:, None, :]
            x1 = x[..., ::2]
            x2 = x[..., 1::2]
            out1 = x1 * cos - x2 * sin
            out2 = x1 * sin + x2 * cos
            return jnp.stack([out1, out2], axis=-1).reshape(x.shape)
        key = jax.random.key(seed)
        k1, k2, k3 = jax.random.split(key, 3)
        batch, seq_len, embed_dim = (2, 1024, 512)
        x = jax.random.normal(k1, (batch, seq_len, embed_dim), dtype=jnp.float32)
        W_qkv = jax.random.normal(k2, (embed_dim, 3 * NUM_HEADS * HEAD_DIM), dtype=jnp.float32) * 0.02
        W_out = jax.random.normal(k3, (NUM_HEADS * HEAD_DIM, embed_dim), dtype=jnp.float32) * 0.02
        return {'x': x, 'W_qkv': W_qkv, 'W_out': W_out}
    _L0_attn_all = _L0_attn_setup()
    _L0_attn_in = {k: v for k, v in _L0_attn_all.items() if k in ('W_qkv', 'W_out')}
    del _L0_attn_all

    def _L0_xattn_setup():
        import jax, jax.numpy as jnp
        import numpy as np
        B, T_Q, T_KV, D = (4, 1024, 2048, 512)
        H = 16
        HD = D // H
        EPS_LN = 1e-05
        EPS_NORM = 1e-12

        def _layernorm(x, g, b):
            mu = jnp.mean(x, axis=-1, keepdims=True)
            var = jnp.mean(jnp.square(x - mu), axis=-1, keepdims=True)
            return (x - mu) * jax.lax.rsqrt(var + EPS_LN) * g + b
        key = jax.random.key(seed)
        ks = jax.random.split(key, 12)
        inp = {'query': jax.random.normal(ks[0], (B, T_Q, D), jnp.float32), 'key': jax.random.normal(ks[1], (B, T_KV, D), jnp.float32), 'value': jax.random.normal(ks[2], (B, T_KV, D), jnp.float32), 'Wq': jax.random.normal(ks[3], (D, D), jnp.float32) * 0.02, 'Wk': jax.random.normal(ks[4], (D, D), jnp.float32) * 0.02, 'Wv': jax.random.normal(ks[5], (D, D), jnp.float32) * 0.02, 'Wo': jax.random.normal(ks[6], (D, D), jnp.float32) * 0.01, 'bo': jnp.zeros((D,), jnp.float32), 'Wbeta': jax.random.normal(ks[7], (H, D), jnp.float32) * 0.02, 'bbeta': jnp.zeros((H,), jnp.float32), 'Walpha': jax.random.normal(ks[8], (H, D), jnp.float32) * 0.02, 'balpha': jnp.full((H,), -1.0, jnp.float32), 'gq': jnp.ones((HD,), jnp.float32), 'bq': jnp.zeros((HD,), jnp.float32), 'gk': jnp.ones((HD,), jnp.float32), 'bk': jnp.zeros((HD,), jnp.float32)}
        return inp
    _L0_xattn_all = _L0_xattn_setup()
    _L0_xattn_in = {k: v for k, v in _L0_xattn_all.items() if k in ('Wq', 'Wk', 'Wv', 'Wo', 'bo', 'Wbeta', 'bbeta', 'Walpha', 'balpha', 'gq', 'bq', 'gk', 'bk')}
    del _L0_xattn_all

    def _L0_ffn_setup():
        import jax, jax.numpy as jnp
        import numpy as np
        EMBED = 512
        NUM_EXPERTS = 8
        TOP_K = 2
        key = jax.random.key(seed)
        ks = jax.random.split(key, 6)
        scale = EMBED ** (-0.5)
        return {'x': jax.random.normal(ks[0], (4, 2048, EMBED), jnp.float32), 'router_w': jax.random.normal(ks[1], (EMBED, NUM_EXPERTS), jnp.float32) * scale, 'router_b': jnp.zeros((NUM_EXPERTS,), jnp.float32), 'we_gate': jax.random.normal(ks[2], (NUM_EXPERTS, EMBED, EMBED), jnp.float32) * scale, 'we_up': jax.random.normal(ks[3], (NUM_EXPERTS, EMBED, EMBED), jnp.float32) * scale, 'we_down': jax.random.normal(ks[4], (NUM_EXPERTS, EMBED, EMBED), jnp.float32) * scale}
    _L0_ffn_all = _L0_ffn_setup()
    _L0_ffn_in = {k: v for k, v in _L0_ffn_all.items() if k in ('router_w', 'router_b', 'we_gate', 'we_up', 'we_down')}
    del _L0_ffn_all
    return {'x': x, 'ctx_1024': ctx_1024, 'L0_attn_W_qkv': _L0_attn_in['W_qkv'], 'L0_attn_W_out': _L0_attn_in['W_out'], 'L0_xattn_Wq': _L0_xattn_in['Wq'], 'L0_xattn_Wk': _L0_xattn_in['Wk'], 'L0_xattn_Wv': _L0_xattn_in['Wv'], 'L0_xattn_Wo': _L0_xattn_in['Wo'], 'L0_xattn_bo': _L0_xattn_in['bo'], 'L0_xattn_Wbeta': _L0_xattn_in['Wbeta'], 'L0_xattn_bbeta': _L0_xattn_in['bbeta'], 'L0_xattn_Walpha': _L0_xattn_in['Walpha'], 'L0_xattn_balpha': _L0_xattn_in['balpha'], 'L0_xattn_gq': _L0_xattn_in['gq'], 'L0_xattn_bq': _L0_xattn_in['bq'], 'L0_xattn_gk': _L0_xattn_in['gk'], 'L0_xattn_bk': _L0_xattn_in['bk'], 'L0_ffn_router_w': _L0_ffn_in['router_w'], 'L0_ffn_router_b': _L0_ffn_in['router_b'], 'L0_ffn_we_gate': _L0_ffn_in['we_gate'], 'L0_ffn_we_up': _L0_ffn_in['we_up'], 'L0_ffn_we_down': _L0_ffn_in['we_down']}

def reference(x, ctx_1024, L0_attn_W_qkv, L0_attn_W_out, L0_xattn_Wq, L0_xattn_Wk, L0_xattn_Wv, L0_xattn_Wo, L0_xattn_bo, L0_xattn_Wbeta, L0_xattn_bbeta, L0_xattn_Walpha, L0_xattn_balpha, L0_xattn_gq, L0_xattn_bq, L0_xattn_gk, L0_xattn_bk, L0_ffn_router_w, L0_ffn_router_b, L0_ffn_we_gate, L0_ffn_we_up, L0_ffn_we_down):
    import jax
    import jax.numpy as jnp

    def _L0_attn_ref(x, W_qkv, W_out):
        import jax, jax.numpy as jnp
        import numpy as np
        NUM_HEADS = 16
        HEAD_DIM = 64
        NEG_INF = -1000000000.0

        def rotary_embedding(x, seq_len, head_dim):
            positions = jnp.arange(seq_len)
            dim_pairs = jnp.arange(0, head_dim, 2)
            freqs = 1.0 / 10000.0 ** (dim_pairs / head_dim)
            angles = positions[:, None] * freqs[None, :]
            cos = jnp.cos(angles)[:, None, :]
            sin = jnp.sin(angles)[:, None, :]
            x1 = x[..., ::2]
            x2 = x[..., 1::2]
            out1 = x1 * cos - x2 * sin
            out2 = x1 * sin + x2 * cos
            return jnp.stack([out1, out2], axis=-1).reshape(x.shape)
        batch, seq_len, embed_dim = x.shape
        qkv = jnp.einsum('bse,ef->bsf', x, W_qkv)
        qkv = qkv.reshape(batch, seq_len, 3, NUM_HEADS, HEAD_DIM)
        q, k, v = (qkv[:, :, 0], qkv[:, :, 1], qkv[:, :, 2])
        q = rotary_embedding(q, seq_len, HEAD_DIM)
        k = rotary_embedding(k, seq_len, HEAD_DIM)
        scale = 1.0 / jnp.sqrt(jnp.asarray(HEAD_DIM, dtype=x.dtype))
        scores = jnp.einsum('bqhd,bkhd->bhqk', q, k) * scale
        mask = jnp.tril(jnp.ones((seq_len, seq_len), dtype=bool))[None, None, :, :]
        scores = jnp.where(mask, scores, NEG_INF)
        weights = jax.nn.softmax(scores, axis=-1)
        out = jnp.einsum('bhqk,bkhd->bqhd', weights, v)
        out = out.reshape(batch, seq_len, NUM_HEADS * HEAD_DIM)
        return jnp.einsum('bsf,fe->bse', out, W_out)

    def _L0_xattn_ref(query, key, value, Wq, Wk, Wv, Wo, bo, Wbeta, bbeta, Walpha, balpha, gq, bq, gk, bk):
        import jax, jax.numpy as jnp
        import numpy as np
        B, T_Q, T_KV, D = (4, 1024, 2048, 512)
        H = 16
        HD = D // H
        EPS_LN = 1e-05
        EPS_NORM = 1e-12

        def _layernorm(x, g, b):
            mu = jnp.mean(x, axis=-1, keepdims=True)
            var = jnp.mean(jnp.square(x - mu), axis=-1, keepdims=True)
            return (x - mu) * jax.lax.rsqrt(var + EPS_LN) * g + b
        Bq, Tq, Dm = query.shape
        Tkv = key.shape[1]
        q = (query @ Wq.T).reshape(Bq, Tq, H, HD)
        k = (key @ Wk.T).reshape(Bq, Tkv, H, HD)
        v = (value @ Wv.T).reshape(Bq, Tkv, H, HD)
        q = _layernorm(q, gq, bq)
        k = _layernorm(k, gk, bk)
        k = k / jnp.maximum(jnp.linalg.norm(k, axis=-1, keepdims=True), EPS_NORM)
        beta = jax.nn.sigmoid(key @ Wbeta.T + bbeta)
        alpha = jax.nn.sigmoid(key @ Walpha.T + balpha)
        k_t = jnp.moveaxis(k, 1, 0)
        v_t = jnp.moveaxis(v, 1, 0)
        b_t = jnp.moveaxis(beta, 1, 0)
        a_t = jnp.moveaxis(alpha, 1, 0)
        M0 = jnp.zeros((Bq, H, HD, HD), query.dtype)

        def step(M, inputs):
            kt, vt, bt, at = inputs
            Mk = jnp.einsum('bhij,bhj->bhi', M, kt)
            erase = at[..., None, None] * jnp.einsum('bhi,bhj->bhij', Mk, kt)
            write = bt[..., None, None] * jnp.einsum('bhi,bhj->bhij', vt, kt)
            return (M - erase + write, None)
        M, _ = jax.lax.scan(step, M0, (k_t, v_t, b_t, a_t))
        out = jnp.einsum('bhij,bthj->bthi', M, q).reshape(Bq, Tq, Dm)
        out = out @ Wo.T + bo
        return out

    def _L0_ffn_ref(x, router_w, router_b, we_gate, we_up, we_down):
        import jax, jax.numpy as jnp
        import numpy as np
        EMBED = 512
        NUM_EXPERTS = 8
        TOP_K = 2
        x_shape = x.shape
        x_flat = x.reshape(-1, x_shape[-1])
        num_tokens = x_flat.shape[0]
        router_logits = x_flat @ router_w + router_b
        topk_weights, topk_indices = jax.lax.top_k(router_logits, k=TOP_K)
        topk_weights = jax.nn.softmax(topk_weights, axis=-1)
        token_idx_mesh = jnp.repeat(jnp.arange(num_tokens), TOP_K)
        expert_idx_mesh = topk_indices.reshape(-1)
        sort_permutation = jnp.argsort(expert_idx_mesh)
        sorted_expert_idx = expert_idx_mesh[sort_permutation]
        sorted_token_idx = token_idx_mesh[sort_permutation]
        group_sizes = jnp.bincount(sorted_expert_idx, length=NUM_EXPERTS)
        sorted_tokens = x_flat[sorted_token_idx]
        ff_gate = jax.lax.ragged_dot(sorted_tokens, we_gate, group_sizes)
        ff_up = jax.lax.ragged_dot(sorted_tokens, we_up, group_sizes)
        activated = jax.nn.silu(ff_gate) * ff_up
        ff_out = jax.lax.ragged_dot(activated, we_down, group_sizes)
        sorted_weights = topk_weights.reshape(-1)[sort_permutation]
        ff_out = ff_out * sorted_weights[:, None]
        output_flat = jnp.zeros_like(x_flat).at[sorted_token_idx].add(ff_out)
        return output_flat.reshape(x_shape)
    x = x + _L0_attn_ref(_layernorm(x, axis=-1), L0_attn_W_qkv, L0_attn_W_out)
    x = x + _L0_xattn_ref(_layernorm(x, axis=-1), ctx_1024, ctx_1024, L0_xattn_Wq, L0_xattn_Wk, L0_xattn_Wv, L0_xattn_Wo, L0_xattn_bo, L0_xattn_Wbeta, L0_xattn_bbeta, L0_xattn_Walpha, L0_xattn_balpha, L0_xattn_gq, L0_xattn_bq, L0_xattn_gk, L0_xattn_bk)
    x = x + _L0_ffn_ref(_layernorm(x, axis=-1), L0_ffn_router_w, L0_ffn_router_b, L0_ffn_we_gate, L0_ffn_we_up, L0_ffn_we_down)
    return x

_drawn_inputs = setup_inputs


def setup_inputs(seed=0):
    import zlib

    import numpy as np

    out = dict(_drawn_inputs(seed))
    spreads = {'L0_xattn_bo': (0.0, 0.1),
     'L0_xattn_bbeta': (0.0, 0.1),
     'L0_xattn_balpha': (-1.0, 0.2),
     'L0_xattn_gq': (1.0, 0.2),
     'L0_xattn_bq': (0.0, 0.1),
     'L0_xattn_gk': (1.0, 0.2),
     'L0_xattn_bk': (0.0, 0.1),
     'L0_ffn_router_b': (0.0, 0.1)}
    factors = {}
    for name, (base, spread) in spreads.items():
        noise = np.random.default_rng([zlib.crc32(name.encode()), seed]).standard_normal(out[name].shape)
        drawn = base * np.exp(spread * noise) if base else spread * noise
        out[name] = jnp.asarray(drawn.astype(out[name].dtype))
    for name, factor in factors.items():
        out[name] = (out[name] * factor).astype(out[name].dtype)
    return out
```

```python
from contextlib import ExitStack

import concourse.bass as bass
from concourse import mybir
import numpy as np

F32 = mybir.dt.float32
F32R = mybir.dt.float32r
BF16 = mybir.dt.bfloat16
I32 = mybir.dt.int32
U32 = mybir.dt.uint32
ALU = mybir.AluOpType
ACT = mybir.ActivationFunctionType
AXX = mybir.AxisListType.X

P = 128
B, T, D = 4, 1024, 512
TOK = B * T
NT = TOK // P
ET = D // P
H, HD = 16, 64
GH = 4
G = H // GH
QT = T // P
GW = 3 * GH * HD
WCOLS = ET * GW
NWT = 6
XH, XD = 16, 32
TC = 64
CT = B * TC // P
NE = 8
BLK = 512
REG = TOK + BLK
NBLK = (2 * TOK) // BLK + NE - 1
EPS = 1e-5
EPS_NORM = 1e-12
MASKED = -1e30


def program(nc, io):
    dram = {}

    def scratch(name, shape, dt):
        dram[name] = nc.dram_tensor("scr_" + name, shape, dt).ap()
        return dram[name]

    scratch("wsplit", (NWT, 2, P, WCOLS), F32)
    scratch("kc", (B * TC, D), F32)
    scratch("vc", (B * TC, D), F32)
    scratch("ba", (B * TC, 2 * XH), F32)
    scratch("mem", (B, XH, XD, XD), F32)
    scratch("attT", (H * HD, TOK), F32)
    scratch("rinv", (H, B, QT, P), F32)
    scratch("x3", (TOK, D), F32)
    scratch("hs", (NE * REG, D), F32)
    scratch("ys", (NBLK * BLK, D), F32)
    scratch("tab", (4, 32), I32)
    with ExitStack() as keep:
        scan = {
            "k2": keep.enter_context(nc.sbuf_tensor("scan_k", [P, TC, XD], F32)),
            "v2": keep.enter_context(nc.sbuf_tensor("scan_v", [P, TC, XD // 2], F32)),
            "ab": keep.enter_context(nc.sbuf_tensor("scan_ab", [P, 2, TC], F32)),
        }
        context_phase(nc, io, dram, scan)
        attention_phase(nc, io, dram, scan)
    with ExitStack() as keep:
        route = {
            "pos": keep.enter_context(nc.sbuf_tensor("pos", [P, NT, 2], I32)),
            "top": keep.enter_context(nc.sbuf_tensor("top", [P, NT, 2], F32)),
            "w": keep.enter_context(nc.sbuf_tensor("w", [P, NT, 2], F32)),
            "tab": keep.enter_context(nc.sbuf_tensor("tab", [P, 4, 32], I32)),
        }
        memory_phase(nc, io, dram, route)
        expert_phase(nc, io, dram, route)
        combine_phase(nc, io, dram, route)


class Room:

    def __init__(self, nc, name):
        self.nc, self.name, self.ctx, self.sems = nc, name, ExitStack(), []

    def __enter__(self):
        return self

    def __exit__(self, *a):
        self.ctx.__exit__(*a)
        if a[0] is None:
            self.nc.clear_and_free_semaphores(self.sems)
            self.nc.all_engine_barrier()

    def sb(self, name, shape, dt=F32):
        return self.ctx.enter_context(self.nc.sbuf_tensor(self.name + name, shape, dt))

    def ps(self, name, shape, dt=F32):
        return self.ctx.enter_context(self.nc.psum_tensor(self.name + name, shape, dt))

    def sem(self, name):
        self.sems.append(self.nc.alloc_semaphore(self.name + name))
        return self.sems[-1]


def wait_alone(eng, sem, value, counter):
    eng.wait_ge(sem, value)
    eng.sem_inc(counter, 1)


class Chain:

    def __init__(self, eng, sem, base=0, counter=None):
        self.eng, self.sem, self.base, self.n, self.counter = eng, sem, base, 0, counter

    def do(self, ins):
        ins.then_inc(self.sem, 1)
        self.n += 1
        return self.n

    def sync(self):
        if self.counter is None:
            self.eng.wait_ge(self.sem, self.base + self.n)
        else:
            wait_alone(self.eng, self.sem, self.base + self.n, self.counter)

    def step(self, ins):
        self.do(ins)
        self.sync()


def context_phase(nc, io, dram, scan):
    with Room(nc, "c_") as rm:
        raw = rm.sb("raw", [P, 2, WCOLS])
        parts = rm.sb("parts", [P, 2, 2, WCOLS], F32R)
        ctx = rm.sb("ctx", [P, CT, D])
        ctxT = rm.sb("ctxT", [P, ET, CT * P])
        wk = rm.sb("wk", [P, ET, D])
        wv = rm.sb("wv", [P, ET, D])
        wg = rm.sb("wg", [P, ET, 2 * XH])
        gb = rm.sb("gb", [P, 2 * XH])
        gk = rm.sb("gk", [P, XD])
        bk = rm.sb("bk", [P, XD])
        ident = rm.sb("ident", [P, P])
        kx = rm.sb("kx", [P, D])
        sq = rm.sb("sq", [P, D])
        kn = rm.sb("kn", [P, CT, D])
        vn = rm.sb("vn", [P, CT, D])
        st = rm.sb("st", [P, 6, XH])
        gt = rm.sb("gt", [P, CT, 2 * XH])
        gt2 = rm.sb("gt2", [P, CT, 2 * XH])
        pT = [rm.ps(f"pT{i}", [P, 512]) for i in range(2)]
        pK = rm.ps("pK", [P, 512])
        pV = rm.ps("pV", [P, 512])
        pG = rm.ps("pG", [P, 512])
        s_in = rm.sem("in")
        s_raw = [rm.sem(f"raw{i}") for i in range(2)]
        s_hi = rm.sem("hi")
        s_lo = rm.sem("lo")
        s_put = [rm.sem(f"put{i}") for i in range(2)]
        s_pk = rm.sem("pk")
        s_tr = rm.sem("tr")
        s_trc = rm.sem("trc")
        s_mm = rm.sem("mm")
        s_v = rm.sem("v")
        s_sq = rm.sem("sq")
        s_dve = rm.sem("dve")
        s_kn = rm.sem("kn")
        s_g1 = rm.sem("g1")
        s_g2 = rm.sem("g2")
        s_g3 = rm.sem("g3")
        s_rt = rm.sem("rt")
        s_rs = rm.sem("rs")
        s_out = rm.sem("out")
        s_scan = rm.sem("scan")
        n_in = 16 * 8
        block = rm.ctx.enter_context(nc.Block())

        @block.sync
        def _(sp):
            sp.dma_start(ctx[:, :, :], io["ctx"].rearrange("(t p) d -> p t d", p=P)).then_inc(s_in, 16)
            for dst, src in ((wk, "wkT"), (wv, "wvT"), (wg, "wgT")):
                sp.dma_start(dst[:, :, :], io[src].rearrange("(e p) n -> p e n", p=P)).then_inc(s_in, 16)
            sp.dma_start(gb[:, :], io["gbias"].partition_broadcast(P)).then_inc(s_in, 16)
            sp.dma_start(gk[:, :], io["gk"].partition_broadcast(P)).then_inc(s_in, 16)
            sp.dma_start(bk[:, :], io["bk"].partition_broadcast(P)).then_inc(s_in, 16)
            sp.dma_start(ident[:, :], io["ident"]).then_inc(s_in, 16)
            for i in range(NWT):
                if i >= 2:
                    sp.wait_ge(s_lo, i - 1)
                sp.dma_start(raw[:, i % 2, :], io["wts"][i]).then_inc(s_raw[i % 2], 16)
                if i >= 1:
                    sp.wait_ge(s_lo, i)
                    sp.dma_start(dram["wsplit"][i - 1].rearrange("a p n -> p a n"),
                                 parts[:, (i - 1) % 2, :, :].bitcast(F32)).then_inc(s_put[(i - 1) % 2], 16)
            sp.wait_ge(s_lo, NWT)
            sp.dma_start(dram["wsplit"][NWT - 1].rearrange("a p n -> p a n"),
                         parts[:, (NWT - 1) % 2, :, :].bitcast(F32)).then_inc(s_put[(NWT - 1) % 2], 16)
            sp.wait_ge(s_kn, CT)
            sp.wait_ge(s_v, CT)
            sp.wait_ge(s_g3, CT)
            for c in range(CT):
                rows = slice(c * P, (c + 1) * P)
                sp.dma_start(dram["kc"][rows, :], kn[:, c, :]).then_inc(s_out, 16)
                sp.dma_start(dram["vc"][rows, :], vn[:, c, :]).then_inc(s_out, 16)
                sp.dma_start(dram["ba"][rows, :], gt[:, c, :]).then_inc(s_out, 16)
            sp.wait_ge(s_out, 16 * 3 * CT)
            n = 0
            for half in range(2):
                for b in range(B):
                    p0 = half * B * XH + b * XH
                    dst = slice(p0, p0 + XH)
                    rows = slice(b * TC, (b + 1) * TC)
                    sp.dma_start(scan["k2"][dst, :, :],
                                 dram["kc"][rows, :].rearrange("t (h j) -> h t j", h=XH)).then_inc(s_scan, 16)
                    v = dram["vc"][rows, :].rearrange("t (h a i) -> h a t i", h=XH, a=2)
                    sp.dma_start(scan["v2"][dst, :, :], v[:, half]).then_inc(s_scan, 16)
                    for a in range(2):
                        sp.dma_start(scan["ab"][dst, a, :],
                                     dram["ba"][rows, a * XH:(a + 1) * XH].rearrange("t h -> h t"),
                                     allow_slow_non_contiguous=True).then_inc(s_scan, 16)
                    n += 4
            sp.wait_ge(s_scan, 16 * n)
            for i in range(2):
                sp.wait_ge(s_put[i], 16 * NWT // 2)

        @block.scalar
        def _(act):
            act.wait_ge(s_in, n_in)
            for c in range(CT):
                act.wait_ge(s_tr, c + 1)
                act.activation(ctxT[:, :, c * P:(c + 1) * P], pT[c][:, :].rearrange("p (e t) -> p e t", e=ET),
                               ACT.Copy).then_inc(s_trc, 1)
            for c in range(CT):
                act.wait_ge(s_mm, 3 * c + 2)
                act.activation(vn[:, c, :], pV[:, :], ACT.Copy).then_inc(s_v, 1)
                for r in range(2):
                    act.wait_ge(s_rt, 2 * c + r + 1)
                    act.activation(st[:, 2 + 2 * r, :], st[:, 1 + 2 * r, :], ACT.Sqrt).then_inc(s_rs, 1)
            for c in range(CT):
                act.wait_ge(s_g1, c + 1)
                act.activation(gt2[:, c, :], gt[:, c, :], ACT.Exp, scale=-1.0).then_inc(s_g2, 1)
            for i in range(NWT):
                act.wait_ge(s_raw[i % 2], 16 * (i // 2 + 1))
                if i >= 2:
                    act.wait_ge(s_put[i % 2], 16 * (i // 2))
                act.activation(parts[:, i % 2, 0, :], raw[:, i % 2, :], ACT.Copy).then_inc(s_hi, 1)

        @block.tensor
        def _(pe):
            pe.wait_ge(s_in, n_in)
            for c in range(CT):
                for e in range(ET):
                    mm = pe.transpose(pT[c][:, e * P:(e + 1) * P], ctx[:, c, e * P:(e + 1) * P], ident[:, :])
                mm.then_inc(s_tr, 1)
            for c in range(CT):
                pe.wait_ge(s_trc, c + 1)
                if c:
                    pe.wait_ge(s_pk, c)
                    pe.wait_ge(s_g1, c)
                    pe.wait_ge(s_v, c)
                for out, w, n in ((pK, wk, D), (pV, wv, D), (pG, wg, 2 * XH)):
                    for e in range(ET):
                        mm = pe.matmul(out[:, 0:n], ctxT[:, e, c * P:(c + 1) * P], w[:, e, :],
                                       start=e == 0, stop=e == ET - 1)
                    mm.then_inc(s_mm, 1)

        @block.vector
        def _(dve):
            ch = Chain(dve, s_dve)
            dve.wait_ge(s_in, n_in)

            def heads(x):
                return x.rearrange("p (h j) -> p h j", h=XH)

            def per_head(x):
                return x.unsqueeze(2).broadcast_to([P, XH, XD])

            def per_dim(x):
                return x[:, :].unsqueeze(1).broadcast_to([P, XH, XD])

            for c in range(CT):
                dve.wait_ge(s_mm, 3 * c + 1)
                ch.step(dve.tensor_reduce(st[:, 0, :], heads(pK[:, :]), AXX, ALU.add))
                ch.step(dve.tensor_scalar(st[:, 0, :], st[:, 0, :], 1.0 / XD, None, ALU.mult))
                dve.tensor_tensor(heads(kx[:, :]), heads(pK[:, :]), per_head(st[:, 0, :]),
                                  ALU.subtract).then_inc(s_pk, 1)
                dve.wait_ge(s_mm, 3 * c + 3)
                dve.tensor_tensor(gt[:, c, :], pG[:, 0:2 * XH], gb[:, :], ALU.add).then_inc(s_g1, 1)
                dve.wait_ge(s_pk, c + 1)
                ch.step(dve.tensor_tensor(sq[:, :], kx[:, :], kx[:, :], ALU.mult))
                ch.step(dve.tensor_reduce(st[:, 1, :], heads(sq[:, :]), AXX, ALU.add))
                dve.tensor_scalar(st[:, 1, :], st[:, 1, :], 1.0 / XD, EPS, ALU.mult, ALU.add).then_inc(s_rt, 1)
                dve.wait_ge(s_rs, 2 * c + 1)
                ch.step(dve.reciprocal(st[:, 5, :], st[:, 2, :]))
                ch.step(dve.tensor_tensor(heads(kx[:, :]), heads(kx[:, :]), per_head(st[:, 5, :]), ALU.mult))
                ch.step(dve.tensor_tensor(heads(kx[:, :]), heads(kx[:, :]), per_dim(gk), ALU.mult))
                ch.step(dve.tensor_tensor(heads(kx[:, :]), heads(kx[:, :]), per_dim(bk), ALU.add))
                ch.step(dve.tensor_tensor(sq[:, :], kx[:, :], kx[:, :], ALU.mult))
                dve.tensor_reduce(st[:, 3, :], heads(sq[:, :]), AXX, ALU.add).then_inc(s_rt, 1)
                dve.wait_ge(s_rs, 2 * c + 2)
                ch.step(dve.tensor_scalar(st[:, 5, :], st[:, 4, :], EPS_NORM, None, ALU.max))
                ch.step(dve.reciprocal(st[:, 5, :], st[:, 5, :]))
                dve.tensor_tensor(heads(kn[:, c, :]), heads(kx[:, :]), per_head(st[:, 5, :]),
                                  ALU.mult).then_inc(s_kn, 1)
                dve.wait_ge(s_kn, c + 1)
            for c in range(CT):
                dve.wait_ge(s_g2, c + 1)
                ch.step(dve.tensor_scalar(gt2[:, c, :], gt2[:, c, :], 1.0, None, ALU.add))
                dve.reciprocal(gt[:, c, :], gt2[:, c, :]).then_inc(s_g3, 1)
            for i in range(NWT):
                dve.wait_ge(s_hi, i + 1)
                dve.tensor_tensor(parts[:, i % 2, 1, :], raw[:, i % 2, :], parts[:, i % 2, 0, :].bitcast(F32),
                                  ALU.subtract).then_inc(s_lo, 1)


def attention_phase(nc, io, dram, scan):
    with Room(nc, "a_") as rm:
        wg = rm.sb("wg", [P, 2, ET, GW], F32R)
        xT = rm.sb("xT", [P, 2, ET, T], F32R)
        cos = rm.sb("cos", [P, T])
        sin = rm.sb("sin", [P, T])
        qs = rm.sb("qs", [P, GH, T], F32R)
        kh = rm.sb("kh", [P, GH, T], F32R)
        kl = rm.sb("kl", [P, GH, T], F32R)
        v2 = rm.sb("v2", [P, QT, GH, 2, HD], F32R)
        pb = rm.sb("pb", [P, 2, T])
        pt = rm.sb("pt", [P, 2, 2, QT, 2 * P], F32R)
        otmp = rm.sb("otmp", [HD, 2, 2 * P])
        ot = rm.sb("ot", [HD, 2, 2 * P])
        xt = rm.sb("xt", [P, 2, D])
        xn = rm.sb("xn", [P, 2, D])
        rsum = rm.sb("rsum", [P, G * GH * QT])
        rT = rm.sb("rT", [P, P])
        nmax = rm.sb("nmax", [P, GH * QT])
        nbias = rm.sb("nbias", [P, GH * QT])
        ident = rm.sb("ident", [P, P])
        identb = rm.sb("identb", [P, P], BF16)
        maskb = rm.sb("maskb", [P, P], BF16)
        bst = rm.sb("bst", [P, 6])
        mv = rm.sb("mv", [P, 2, 2])
        sd = rm.sb("sd", [P, 2])
        rstd = rm.sb("rstd", [P, 2])
        eps = rm.sb("eps", [P, 1])
        ptf = pt[:, :, :, :, :].rearrange("p a b c d -> p (a b c d)")
        rot = [ptf[:, i * 4 * T:(i + 1) * 4 * T].rearrange("p (r t) -> p r t", r=4) for i in range(2)]
        tmp = pb[:, :, :].rearrange("p a (b t) -> p (a b) t", b=2)

        S = [rm.ps(f"S{i}", [P, T]) for i in range(2)]
        PT = [rm.ps(f"PT{i}", [P, 512]) for i in range(2)]
        O = [rm.ps(f"O{i}", [P, 512]) for i in range(2)]

        M = rm.sb("M", [P, XD // 2, XD])
        sp1 = rm.sb("sp1", [P, XD // 2, XD])
        bv = rm.sb("bv", [P, TC, XD // 2])
        coef = rm.sb("coef", [P, XD // 2])
        s_sc = rm.sem("sc")
        s_mem = rm.sem("mem")

        s_any = rm.sem("any")
        s_const = rm.sem("const")
        s_pool = rm.sem("pool")
        s_w = rm.sem("w")
        s_x = [rm.sem(f"x{i}") for i in range(2)]
        s_bn = rm.sem("bn")
        s_mv = rm.sem("mv")
        s_sd = rm.sem("sd")
        s_rstd = rm.sem("rstd")
        s_xn = rm.sem("xn")
        s_xT = rm.sem("xT")
        s_ptfull = rm.sem("ptfull")
        s_pthi = rm.sem("pthi")
        s_ptfree = rm.sem("ptfree")
        s_sfull = rm.sem("sfull")
        s_rel = rm.sem("rel")
        s_rop = rm.sem("rop")
        s_rhi = rm.sem("rhi")
        s_rot = rm.sem("rot")
        s_vhi = rm.sem("vhi")
        s_vlo = rm.sem("vlo")
        s_stack = [rm.sem(f"stack{i}") for i in range(GH)]
        s_max = rm.sem("max")
        s_nb = rm.sem("nb")
        s_exp = rm.sem("exp")
        s_pv = rm.sem("pv")
        s_oc = rm.sem("oc")
        s_ofree = rm.sem("ofree")
        s_ost = [rm.sem(f"ost{i}") for i in range(2)]
        s_rsT = rm.sem("rsT")
        s_rinv = rm.sem("rinv")
        s_rst = rm.sem("rst")

        NP_ = GH * QT // 2
        NS = 6 + GH * QT
        uses = [(qt // 4) + 1 for qt in range(QT)]
        NPT = GH * sum(uses)
        PTB = QT + G * NPT
        CREDIT = 2

        def pt_index(u):
            h, qt = u // QT, u % QT
            return h * sum(uses) + sum(uses[:qt])

        block = rm.ctx.enter_context(nc.Block())

        @block.sync
        def _(sp):
            sp.dma_start(cos[:, :], io["cos"]).then_inc(s_const, 16)
            sp.dma_start(sin[:, :], io["sin"]).then_inc(s_const, 16)
            sp.dma_start(ident[:, :], io["ident"]).then_inc(s_const, 16)
            sp.dma_start(wg[:, :, :, :].rearrange("p a e n -> p a (e n)").bitcast(F32),
                         dram["wsplit"][0].rearrange("a p n -> p a n")).then_inc(s_w, 16)
            with sp.Fori(0, B) as b:
                for t in range(QT):
                    wait_alone(sp, s_xn, b * QT + t - 2 + 1 + CREDIT, s_any)
                    sp.dma_start(xt[:, t % 2, :], io["x"][bass.ds(b * T + t * P, P), :]).then_inc(s_x[t % 2], 16)
                with sp.Fori(0, G) as g:
                    n = b * G + g
                    wait_alone(sp, s_rot, 4 * n + 2, s_any)
                    for h in range(GH):
                        src = slice(h * 32, h * 32 + 32)
                        for r in range(4):
                            sp.dma_start(qs[r * 32:r * 32 + 32, h, :].bitcast(F32),
                                         rot[0][src, r, :].bitcast(F32)).then_inc(s_stack[h], 16)
                    wait_alone(sp, s_rot, 4 * n + 4, s_any)
                    for h in range(GH):
                        src = slice(h * 32, h * 32 + 32)
                        for r in range(4):
                            dst = (kh, kl)[r // 2]
                            for dup in range(2):
                                p0 = dup * 64 + (r % 2) * 32
                                sp.dma_start(dst[p0:p0 + 32, h, :].bitcast(F32),
                                             rot[1][src, r, :].bitcast(F32)).then_inc(s_stack[h], 16)
                    wait_alone(sp, s_sfull, n * NS + 6, s_any)
                    sp.dma_start(wg[:, :, :, :].rearrange("p a e n -> p a (e n)").bitcast(F32),
                                 dram["wsplit"][bass.ds((g + 1) % G, 1)].rearrange("o a p n -> p (o a) n")
                                 ).then_inc(s_w, 16)
                    for k in range(NP_):
                        h, pr = k // (QT // 2), k % (QT // 2)
                        wait_alone(sp, s_ofree, n * NP_ + k + 1 + CREDIT, s_any)
                        sp.dma_start(dram["attT"][bass.ds(g * GH * HD + h * HD, HD),
                                                  bass.ds(b * T + pr * 2 * P, 2 * P)],
                                     ot[:, k % 2, :]).then_inc(s_ost[k % 2], 16)
                wait_alone(sp, s_rinv, b + 1, s_any)
                for g in range(G):
                    sp.dma_start(dram["rinv"][g * GH:(g + 1) * GH, bass.ds(b, 1), :, :]
                                 .rearrange("h o q p -> h (o q) p"),
                                 rT[g * GH * QT:(g + 1) * GH * QT, :]).then_inc(s_rst, 16)
            sp.wait_ge(s_rst, 16 * (G * B + 1))
            sp.wait_ge(s_w, 16 * (B * G + 1))
            for i in range(2):
                sp.wait_ge(s_ost[i], 16 * (B * G * NP_ // 2 + 1))

        @block.gpsimd
        def _(gp):
            gp.memset(identb[:, :], 0.0).then_inc(s_pool, 1)
            gp.memset(maskb[:, :], 0.0).then_inc(s_pool, 1)
            gp.memset(eps[:, :], EPS).then_inc(s_pool, 1)
            gp.wait_ge(s_pool, 3)
            gp.affine_select(out=identb[:, :], in_=identb[:, :], compare_op=ALU.not_equal, fill=1.0,
                             base=0, pattern=[[-1, P]], channel_multiplier=1).then_inc(s_pool, 1)
            gp.affine_select(out=maskb[:, :], in_=maskb[:, :], compare_op=ALU.is_ge, fill=MASKED,
                             base=0, pattern=[[-1, P]], channel_multiplier=1).then_inc(s_pool, 1)
            ch = Chain(gp, s_sc)
            half = XD // 2
            ch.do(gp.memset(M[:, :, :], 0.0))
            ch.step(gp.tensor_tensor(bv[:, :, :], scan["v2"][:, :, :],
                                     scan["ab"][:, 0, :].unsqueeze(2).broadcast_to([P, TC, half]), ALU.mult))
            per = 10
            with gp.Fori(0, TC) as t:
                c = Chain(gp, s_sc, t * per + ch.n, s_any)
                kt = scan["k2"][:, bass.ds(t, 1), :].broadcast_to([P, half, XD])
                c.step(gp.tensor_tensor(sp1[:, :, :], M[:, :, :], kt, ALU.mult))
                w = XD // 2
                while w:
                    c.step(gp.tensor_tensor(sp1[:, :, 0:w], sp1[:, :, 0:w], sp1[:, :, w:2 * w], ALU.add))
                    w //= 2
                c.step(gp.tensor_tensor(coef[:, :].unsqueeze(2), sp1[:, :, 0:1],
                                        scan["ab"][:, 1, bass.ds(t, 1)].unsqueeze(1).broadcast_to([P, half, 1]),
                                        ALU.mult))
                c.step(gp.tensor_tensor(coef[:, :].unsqueeze(1), bv[:, bass.ds(t, 1), :],
                                        coef[:, :].unsqueeze(1), ALU.subtract))
                c.step(gp.tensor_tensor(sp1[:, :, :], kt, coef[:, :].unsqueeze(2).broadcast_to([P, half, XD]),
                                        ALU.mult))
                c.step(gp.tensor_tensor(M[:, :, :], M[:, :, :], sp1[:, :, :], ALU.add))
                assert c.n == per
            for a in range(2):
                gp.dma_start(dram["mem"][:, :, a * half:(a + 1) * half, :].rearrange("b h i j -> (b h) (i j)"),
                             M[a * 64:(a + 1) * 64, :, :].rearrange("p i j -> p (i j)")).then_inc(s_mem, 16)
            gp.wait_ge(s_mem, 32)

        @block.tensor
        def _(pe):
            pe.sem_inc(s_pv, CREDIT)
            pe.wait_ge(s_const, 48)
            pe.wait_ge(s_pool, 5)

            def split_mm(out, lhs, rhs, start, stop):
                pe.matmul(out, lhs(0), rhs(0), start=start, stop=False)
                pe.matmul(out, lhs(0), rhs(1), start=False, stop=False)
                return pe.matmul(out, lhs(1), rhs(0), start=False, stop=stop)

            with pe.Fori(0, B) as b:
                for t in range(QT):
                    pe.wait_ge(s_xn, b * QT + t + 1 + CREDIT)
                    pe.wait_ge(s_ptfree, b * PTB + t + 1)
                    for e in range(ET):
                        mm = pe.transpose(PT[t % 2][:, e * P:(e + 1) * P], xn[:, t % 2, e * P:(e + 1) * P],
                                          ident[:, :])
                    mm.then_inc(s_ptfull, 1)
                with pe.Fori(0, G) as g:
                    n = b * G + g
                    pt0 = b * PTB + QT + g * NPT
                    pe.wait_ge(s_w, 16 * (n + 1))
                    for j in range(4):
                        col0, c = (j // 2) * 2 * P, j % 2
                        if j < 2:
                            pe.wait_ge(s_exp, 32 * n + j - 1 + CREDIT)
                        else:
                            pe.wait_ge(s_rel, 6 * n + j - 1)
                        if j == 0:
                            pe.wait_ge(s_xT, (b + 1) * QT)
                        for a in range(2):
                            for e in range(ET):
                                mm = split_mm(S[j % 2][:, a * 512:(a + 1) * 512],
                                              lambda i: wg[:, i, e, col0 + a * P:col0 + (a + 1) * P],
                                              lambda i: xT[:, i, e, c * 512:(c + 1) * 512],
                                              e == 0, e == ET - 1)
                        mm.then_inc(s_sfull, 1)
                    for j in range(4, 6):
                        pe.wait_ge(s_rel, 6 * n + j - 1)
                        for tt in range(4):
                            t = (j - 4) * 4 + tt
                            for e in range(ET):
                                mm = split_mm(S[j % 2][:, tt * 256:(tt + 1) * 256],
                                              lambda i: xT[:, i, e, t * P:(t + 1) * P],
                                              lambda i: wg[:, i, e, 4 * P:6 * P],
                                              e == 0, e == ET - 1)
                        mm.then_inc(s_sfull, 1)

                    def scores(u):
                        h, qt = u // QT, u % QT
                        if qt == 0:
                            pe.wait_ge(s_stack[h], 16 * 12 * (n + 1))
                        if u < 2:
                            pe.wait_ge(s_rel, 6 * n + 4 + u + 1)
                        else:
                            pe.wait_ge(s_exp, 32 * n + u - 1 + CREDIT)
                        q = qs[:, h, qt * P:(qt + 1) * P]
                        cols = (qt + 1) * P
                        for c0 in range(0, cols, 512):
                            c1 = min(cols, c0 + 512)
                            out = S[u % 2][:, c0:c1]
                            last = c1 == cols
                            pe.matmul(out, q, kh[:, h, c0:c1], start=True, stop=False)
                            mm = pe.matmul(out, q, kl[:, h, c0:c1], start=False, stop=not last)
                        mm = pe.matmul(S[u % 2][:, cols - P:cols], identb[:, :], maskb[:, :],
                                       start=False, stop=True)
                        mm.then_inc(s_sfull, 1)

                    def turn(u):
                        h, qt = u // QT, u % QT
                        pe.wait_ge(s_exp, 32 * n + u + 1 + CREDIT)
                        k = pt_index(u)
                        for s in range(uses[qt]):
                            pe.wait_ge(s_ptfree, pt0 + k + s + 1)
                            for kt in range(4 * s, min(qt + 1, 4 * s + 4)):
                                mm = pe.transpose(PT[(k + s) % 2][:, (kt % 4) * P:(kt % 4 + 1) * P],
                                                  pb[:, u % 2, kt * P:(kt + 1) * P], ident[:, :])
                            mm.then_inc(s_ptfull, 1)

                    def values(k, part):
                        h, pr = k // (QT // 2), k % (QT // 2)
                        if part == 0:
                            last = pt_index(2 * k + 1) + uses[(2 * k + 1) % QT]
                            pe.wait_ge(s_ptfree, pt0 + last + CREDIT)
                            pe.wait_ge(s_ofree, n * NP_ + k + 1)
                            if k == 0:
                                pe.wait_ge(s_vlo, 2 * (n + 1))
                        nk = 2 * pr + 2
                        for kt in range(nk):
                            c0 = P if kt == nk - 1 else 0
                            mm = pe.matmul(O[k % 2][:, c0:2 * P],
                                           v2[:, kt, h, :, :].rearrange("p a d -> p (a d)"),
                                           pt[:, k % 2, part, kt, c0:2 * P],
                                           start=kt == 0 and part == 0, stop=kt == nk - 1 and part == 1)
                        if part == 1:
                            mm.then_inc(s_pv, 1)

                    for u in range(GH * QT + 4):
                        if 2 <= u < GH * QT + 2:
                            turn(u - 2)
                        if u < GH * QT:
                            scores(u)
                        if u >= 4:
                            values((u - 4) // 2, u % 2)
                pe.wait_ge(s_ofree, (b + 1) * G * NP_ + CREDIT)
                pe.wait_ge(s_exp, (b + 1) * G * 32 + CREDIT)
                pe.transpose(O[0][:, 0:P], rsum[:, :], ident[:, :]).then_inc(s_rsT, 1)
                pe.wait_ge(s_rinv, b + 1)

        @block.scalar
        def _(act):
            act.sem_inc(s_exp, CREDIT)
            act.wait_ge(s_pool, 5)
            with act.Fori(0, B) as b:
                def ln_scale(t):
                    act.wait_ge(s_mv, b * QT + t + 1)
                    act.activation(sd[:, t % 2:t % 2 + 1], mv[:, t % 2, 1:2], ACT.Sqrt, bias=eps[:, 0:1],
                                   scale=1.0).then_inc(s_sd, 1)

                ln_scale(0)
                for t in range(QT):
                    if t + 1 < QT:
                        ln_scale(t + 1)
                    act.wait_ge(s_ptfull, b * PTB + t + 1)
                    act.activation(xT[:, 0, :, t * P:(t + 1) * P], PT[t % 2][:, :].rearrange("p (e t) -> p e t", e=ET),
                                   ACT.Copy).then_inc(s_pthi, 1)
                with act.Fori(0, G) as g:
                    n = b * G + g
                    pt0 = b * PTB + QT + g * NPT
                    for j in range(4):
                        for r in range(2):
                            act.wait_ge(s_rop, n * 24 + j * 6 + 3 * r + 3)
                            act.activation(rot[j // 2][:, r, (j % 2) * 512:(j % 2 + 1) * 512],
                                           tmp[:, 2 * r, :], ACT.Copy).then_inc(s_rhi, 1)
                    for j in range(2):
                        act.wait_ge(s_sfull, n * NS + 5 + j)
                        act.activation(v2[:, 4 * j:4 * j + 4, :, 0, :],
                                       S[j % 2][:, :].rearrange("p (t h d) -> p t h d", t=4, h=GH),
                                       ACT.Copy).then_inc(s_vhi, 1)

                    def exps(u):
                        h, qt = u // QT, u % QT
                        act.wait_ge(s_nb, 32 * n + u + 1)
                        if u < 2:
                            act.wait_ge(s_rot, 4 * (n + 1))
                        else:
                            act.wait_ge(s_ptfull, pt0 + pt_index(u - 2) + uses[(u - 2) % QT])
                        cols = (qt + 1) * P
                        act.activation(pb[:, u % 2, 0:cols], S[u % 2][:, 0:cols], ACT.Exp,
                                       bias=nbias[:, u:u + 1], scale=HD ** -0.5,
                                       accum_out=rsum[:, bass.ds(g * GH * QT + u, 1)]).then_inc(s_exp, 1)

                    def part_high(u):
                        h, qt = u // QT, u % QT
                        k = pt_index(u)
                        if u == 0:
                            for i in range(GH):
                                act.wait_ge(s_stack[i], 16 * 12 * (n + 1))
                        if u % 2 == 0:
                            act.wait_ge(s_pv, NP_ * n + u // 2 - 1 + CREDIT)
                        for s in range(uses[qt]):
                            m = min(4, qt + 1 - 4 * s)
                            act.wait_ge(s_ptfull, pt0 + k + s + 1)
                            act.activation(pt[:, (u // 2) % 2, 0, 4 * s:4 * s + m, (u % 2) * P:(u % 2 + 1) * P],
                                           PT[(k + s) % 2][:, 0:m * P].rearrange("p (k q) -> p k q", k=m),
                                           ACT.Copy).then_inc(s_pthi, 1)

                    def out_low(k):
                        act.wait_ge(s_pv, NP_ * n + k + 1 + CREDIT)
                        act.wait_ge(s_ofree, n * NP_ + k + 1)
                        act.activation(otmp[:, k % 2, :], O[k % 2][HD:P, 0:2 * P], ACT.Copy).then_inc(s_oc, 1)

                    for u in range(GH * QT + 6):
                        if 2 <= u < GH * QT + 2:
                            part_high(u - 2)
                        if u < GH * QT:
                            exps(u)
                        if u >= 6 and u % 2 == 1:
                            out_low((u - 6) // 2)
                    

        @block.vector
        def _(dve):
            dve.sem_inc(s_ptfree, CREDIT)
            dve.sem_inc(s_ofree, CREDIT)
            dve.sem_inc(s_xn, CREDIT)
            dve.sem_inc(s_ost[0], 16)
            dve.sem_inc(s_ost[1], 16)
            dve.sem_inc(s_rst, 16)
            dve.wait_ge(s_const, 48)
            with dve.Fori(0, B) as b:
                def stats(t):
                    i = b * QT + t
                    dve.wait_ge(s_x[t % 2], b * (16 * QT // 2) + 16 * (t // 2 + 1))
                    dve.bn_stats(bst[:, :], xt[:, t % 2, :]).then_inc(s_bn, 1)
                    wait_alone(dve, s_bn, i + 1, s_any)
                    dve.bn_aggr(mv[:, t % 2, :], bst[:, :]).then_inc(s_mv, 1)
                    dve.wait_ge(s_mv, i + 1)

                def normalise(t):
                    i = b * QT + t
                    dve.wait_ge(s_sd, i + 1)
                    dve.reciprocal(rstd[:, t % 2:t % 2 + 1], sd[:, t % 2:t % 2 + 1]).then_inc(s_rstd, 1)
                    dve.wait_ge(s_rstd, i + 1)
                    if t >= 2:
                        dve.wait_ge(s_ptfull, b * PTB + t - 1)
                    dve.tensor_scalar(xn[:, t % 2, :], xt[:, t % 2, :], mv[:, t % 2, 0:1],
                                      rstd[:, t % 2:t % 2 + 1], ALU.subtract, ALU.mult).then_inc(s_xn, 1)
                    dve.wait_ge(s_xn, i + 1 + CREDIT)

                def x_low(t):
                    dve.wait_ge(s_pthi, b * PTB + t + 1)
                    lo = xT[:, 1, :, t * P:(t + 1) * P]
                    dve.tensor_tensor(lo, PT[t % 2][:, :].rearrange("p (e t) -> p e t", e=ET),
                                      xT[:, 0, :, t * P:(t + 1) * P].bitcast(F32), ALU.subtract
                                      ).then_inc(s_ptfree, 1)
                    dve.wait_ge(s_ptfree, b * PTB + t + 1 + CREDIT)
                    dve.sem_inc(s_xT, 1)

                stats(0)
                for t in range(QT):
                    if t + 1 < QT:
                        stats(t + 1)
                    normalise(t)
                    if t >= 1:
                        x_low(t - 1)
                x_low(QT - 1)
                with dve.Fori(0, G) as g:
                    n = b * G + g
                    pt0 = b * PTB + QT + g * NPT
                    for j in range(4):
                        c = j % 2
                        cs, sn = cos[:, c * 512:(c + 1) * 512], sin[:, c * 512:(c + 1) * 512]
                        x1, x2 = S[j % 2][:, 0:512], S[j % 2][:, 512:1024]
                        dve.wait_ge(s_sfull, n * NS + j + 1)
                        r0 = n * 24 + j * 6
                        dve.tensor_tensor(tmp[:, 0, :], x1, cs, ALU.mult).then_inc(s_rop, 1)
                        dve.tensor_tensor(tmp[:, 1, :], x2, sn, ALU.mult).then_inc(s_rop, 1)
                        dve.wait_ge(s_rop, r0 + 2)
                        dve.tensor_tensor(tmp[:, 0, :], tmp[:, 0, :], tmp[:, 1, :], ALU.subtract).then_inc(s_rop, 1)
                        dve.tensor_tensor(tmp[:, 2, :], x1, sn, ALU.mult).then_inc(s_rop, 1)
                        dve.tensor_tensor(tmp[:, 3, :], x2, cs, ALU.mult).then_inc(s_rop, 1)
                        dve.wait_ge(s_rop, r0 + 5)
                        dve.sem_inc(s_rel, 1)
                        dve.tensor_tensor(tmp[:, 2, :], tmp[:, 2, :], tmp[:, 3, :], ALU.add).then_inc(s_rop, 1)
                        for r in range(2):
                            dve.wait_ge(s_rhi, n * 8 + j * 2 + r + 1)
                            o = slice(c * 512, (c + 1) * 512)
                            ins = dve.tensor_tensor(rot[j // 2][:, 2 + r, o], tmp[:, 2 * r, :],
                                                    rot[j // 2][:, r, o].bitcast(F32), ALU.subtract)
                        ins.then_inc(s_rot, 1)
                        dve.wait_ge(s_rot, 4 * n + j + 1)
                    for j in range(2):
                        dve.wait_ge(s_vhi, 2 * n + j + 1)
                        src = S[j % 2][:, :].rearrange("p (t h d) -> p t h d", t=4, h=GH)
                        dve.tensor_tensor(v2[:, 4 * j:4 * j + 4, :, 1, :], src,
                                          v2[:, 4 * j:4 * j + 4, :, 0, :].bitcast(F32),
                                          ALU.subtract).then_inc(s_vlo, 1)
                        dve.wait_ge(s_vlo, 2 * n + j + 1)
                        dve.sem_inc(s_rel, 1)

                    def rowmax(u):
                        cols = (u % QT + 1) * P
                        dve.wait_ge(s_sfull, n * NS + 6 + u + 1)
                        dve.tensor_reduce(nmax[:, u:u + 1], S[u % 2][:, 0:cols], AXX, ALU.max).then_inc(s_max, 1)
                        dve.wait_ge(s_max, 32 * n + u + 1)
                        dve.tensor_scalar(nbias[:, u:u + 1], nmax[:, u:u + 1], -(HD ** -0.5), None,
                                          ALU.mult).then_inc(s_nb, 1)

                    def part_low(u):
                        h, qt = u // QT, u % QT
                        k = pt_index(u)
                        for s in range(uses[qt]):
                            m = min(4, qt + 1 - 4 * s)
                            dve.wait_ge(s_pthi, pt0 + k + s + 1)
                            q = slice((u % 2) * P, (u % 2 + 1) * P)
                            dve.tensor_tensor(pt[:, (u // 2) % 2, 1, 4 * s:4 * s + m, q],
                                              PT[(k + s) % 2][:, 0:m * P].rearrange("p (k q) -> p k q", k=m),
                                              pt[:, (u // 2) % 2, 0, 4 * s:4 * s + m, q].bitcast(F32),
                                              ALU.subtract).then_inc(s_ptfree, 1)

                    def out_sum(k):
                        dve.wait_ge(s_oc, n * NP_ + k + 1)
                        dve.wait_ge(s_ost[k % 2], 16 * (NP_ // 2 * n + k // 2) + 16)
                        dve.tensor_tensor(ot[:, k % 2, :], O[k % 2][0:HD, 0:2 * P], otmp[:, k % 2, :],
                                          ALU.add).then_inc(s_ofree, 1)

                    for u in range(GH * QT + 6):
                        if u < GH * QT:
                            rowmax(u)
                        if 2 <= u < GH * QT + 2:
                            part_low(u - 2)
                        if u >= 6 and u % 2 == 1:
                            out_sum((u - 6) // 2)
                dve.wait_ge(s_rsT, b + 1)
                dve.wait_ge(s_rst, 16 * G * b + 16)
                dve.reciprocal(rT[:, :], O[0][:, 0:P]).then_inc(s_rinv, 1)


def memory_phase(nc, io, dram, route):
    with Room(nc, "m_") as rm:
        ww = rm.sb("ww", [P, 2, 2 * WCOLS], F32R)
        mw = rm.sb("mw", [P, 2, ET, D], F32R)
        bd = rm.sb("bd", [P, XH // 4, P])
        wo = rm.sb("wo", [P, ET, D])
        att = rm.sb("att", [P, 2, 8, P])
        rb = rm.sb("rb", [P, 2, 8, P])
        ap = rm.sb("ap", [P, 2, 2, 8, P], F32R)
        x = rm.sb("x", [P, 2, D])
        x2 = rm.sb("x2", [P, 2, D])
        x2b = rm.sb("x2b", [P, 4, D])
        n2 = rm.sb("n2", [P, 2, D])
        nT = rm.sb("nT", [P, 2, 2, ET, P], F32R)
        qc = rm.sb("qc", [P, 2, D])
        sq = rm.sb("sq", [P, D])
        qn = rm.sb("qn", [P, 2, D])
        qf = rm.sb("qf", [P, D])
        qT = rm.sb("qT", [P, 2, 2, ET, P], F32R)
        x3 = rm.sb("x3", [P, 2, D])
        hn = rm.sb("hn", [P, QT, D])
        hT = rm.sb("hT", [P, 2, ET, P])
        rw = rm.sb("rw", [P, ET, NE])
        rbias = rm.sb("rbias", [P, NE])
        bo = rm.sb("bo", [P, D])
        gq = rm.sb("gq", [P, 1])
        bq = rm.sb("bq", [P, 1])
        ident = rm.sb("ident", [P, P])
        zero = rm.sb("zero", [P, D])
        eps = rm.sb("eps", [P, 1])
        tri = rm.sb("tri", [P, P], BF16)
        ones = rm.sb("ones", [P, P], BF16)
        iota8 = rm.sb("iota8", [P, NE])
        base = rm.sb("base", [P, NE])
        it = rm.sb("it", [P, 32], I32)
        itf = rm.sb("itf", [P, 32])
        st = rm.sb("st", [P, 2, 6])
        mv = rm.sb("mv", [P, 2, 2])
        sd = rm.sb("sd", [P, 2])
        rs = rm.sb("rs", [P, 2])
        hs1 = rm.sb("hs1", [P, 2, XH])
        hs2 = rm.sb("hs2", [P, 2, XH])
        hs3 = rm.sb("hs3", [P, 2, XH])
        lg = rm.sb("lg", [P, NE])
        top8 = rm.sb("top8", [P, QT, NE])
        ix8 = rm.sb("ix8", [P, NE], U32)
        idx = rm.sb("idx", [P, 2, NE])
        m1 = rm.sb("m1", [P, NE])
        msum = rm.sb("msum", [P, 2, NE], BF16)
        cum = rm.sb("cum", [P, NE], BF16)
        pr = rm.sb("pr", [P, NE])
        junk = rm.sb("junk", [P, NE])
        pf = rm.sb("pf", [P, 2, 2])
        pi = rm.sb("pi", [P, QT, 2], I32)
        cnt = rm.sb("cnt", [P, NE])
        nb = rm.sb("nb", [P, NE])
        end = rm.sb("end", [P, NE])
        tb = rm.sb("tb", [P, 8, 32])
        e2 = rm.sb("e2", [P, NT])
        tp = rm.sb("tp", [P, 3, 2 * NT])
        pA = [rm.ps(f"A{i}", [P, 512]) for i in range(2)]
        pQ, pM, pR, pW = (rm.ps(n, [P, 512]) for n in "QMRW")
        pT = [rm.ps(f"T{i}", [P, 512]) for i in range(2)]

        names = ("any c dc w bd pool mwp mwh mwl attl0 attl1 xl0 xl1 an ahi alo A x2 bn mv sd rs n2 T nhi nlo Q "
                 "hred hmean qc sq hvar hsd hrs qn qf qhi qlo M x3 hn x2b hT R rt ms rank pos cumd keep tb tot st30 st31 sc0 sc1 sc2 "
                 "sc3 scd cnt e fin zero").split()
        s = {k: rm.sem(k) for k in names}
        CR = 2
        NS = QT + 4
        turns = [(k, i - d) for i in range(NS) for k, d in (("n", 1), ("q", 2), ("h", 3)) if 0 <= i - d < QT]
        done = {"n": "nlo", "q": "qf", "h": "hT"}

        def wait_turn(eng, b, kind, i):
            u = turns.index((kind, i)) - 2
            k, j = turns[u]
            eng.wait_ge(s[done[k]], (b if u >= 0 else b - 1) * QT + j + 1 + CR)

        def slot(kind, i):
            return turns.index((kind, i)) % 2

        order = [(i, k) for i in range(NS) for k in range(2) if 0 <= i - 2 * k < QT]

        def lnorm(b, i, k):
            return b * 2 * QT + order.index((i, k)) + 1

        block = rm.ctx.enter_context(nc.Block())

        @block.sync
        def _(sp):
            for i in range(2):
                sp.dma_start(ww[:, :, i * WCOLS:(i + 1) * WCOLS].bitcast(F32),
                             dram["wsplit"][G + i].rearrange("a p n -> p a n")).then_inc(s["w"], 16)
            for dst, src in ((wo[:, :, :], io["woT"].rearrange("(e p) n -> p e n", p=P)),
                             (rw[:, :, :], io["rw"].rearrange("(e p) n -> p e n", p=P)),
                             (rbias[:, :], io["rb"].partition_broadcast(P)),
                             (bo[:, :], io["bo"].partition_broadcast(P)),
                             (gq[:, :], io["gq"]), (bq[:, :], io["bq"]), (ident[:, :], io["ident"])):
                sp.dma_start(dst, src).then_inc(s["c"], 16)
            sp.wait_ge(s["pool"], 6)
            with sp.Fori(0, B) as b:
                wait_alone(sp, s["mwp"], 4 * b + CR, s["any"])
                for h in range(4):
                    src = dram["mem"][bass.ds(b, 1)].rearrange("o (q h) i j -> h (o i) q j", h=4)[h]
                    sp.dma_start(bd[32 * h:32 * h + 32, :, 32 * h:32 * h + 32], src).then_inc(s["bd"], 16)

                def load(i):
                    wait_alone(sp, s["ahi"], b * QT + i - 1 + CR, s["any"])
                    wait_alone(sp, s["alo"], b * QT + i - 1 + CR, s["any"])
                    wait_alone(sp, s["x2"], b * QT + i - 1 + CR, s["any"])
                    t0 = b * T + i * P
                    a = dram["attT"][:, bass.ds(t0, P)].rearrange("(f p) t -> p f t", p=P)
                    sp.dma_start(att[:, i % 2, :, :], a).then_inc(s[f"attl{i % 2}"], 16)
                    r = dram["rinv"][:, bass.ds(b, 1), i, :].rearrange("(f a) o p -> a (o f) p", a=2)
                    for a in range(2):
                        sp.dma_start(rb[a * 64:(a + 1) * 64, i % 2, :, :],
                                     r[a].partition_broadcast(64)).then_inc(s[f"attl{i % 2}"], 16)
                    sp.dma_start(x[:, i % 2, :], io["x"][bass.ds(t0, P), :]).then_inc(s[f"xl{i % 2}"], 16)

                load(0)
                for i in range(NS):
                    if i + 1 < QT:
                        load(i + 1)
                    if 0 <= i - 2 < QT:
                        wait_alone(sp, s["x3"], b * QT + i - 2 + 1 + CR, s["any"])
                        sp.dma_start(dram["x3"][bass.ds(b * T + (i - 2) * P, P), :],
                                     x3[:, i % 2, :]).then_inc(s[f"st3{i % 2}"], 16)
            for i in range(2):
                sp.wait_ge(s[f"st3{i}"], 16 * (B * QT // 2 + 1))
            sp.wait_ge(s["fin"], 1)
            for e in range(NE):
                z = sp.value_load(route["tab"][0:1, 3, e:e + 1], min_val=0, max_val=(NE - 1) * REG + TOK)
                sp.dma_start(dram["hs"][bass.ds(z, BLK), :].rearrange("(a p) d -> p a d", p=P),
                             zero[:, :].unsqueeze(1).broadcast_to([P, BLK // P, D])).then_inc(s["zero"], 16)
            sp.wait_ge(s["zero"], 16 * NE)

        @block.gpsimd
        def _(gp):
            pool = Chain(gp, s["pool"])
            pool.do(gp.memset(bd[:, :, :], 0.0))
            pool.do(gp.memset(zero[:, :], 0.0))
            pool.do(gp.memset(eps[:, :], EPS))
            pool.do(gp.memset(tri[:, :], 1.0))
            pool.do(gp.memset(ones[:, :], 1.0))
            pool.do(gp.memset(cum[:, :], 0.0))
            pool.do(gp.iota(it[:, :], pattern=[[1, 32]], base=0, channel_multiplier=0))
            pool.sync()
            pool.do(gp.affine_select(out=tri[:, :], in_=tri[:, :], compare_op=ALU.is_ge, fill=0.0,
                                     base=-1, pattern=[[1, P]], channel_multiplier=-1))
            pool.step(gp.tensor_copy(itf[:, :], it[:, :]))
            pool.do(gp.tensor_copy(iota8[:, :], itf[:, 0:NE]))
            pool.step(gp.tensor_scalar(base[:, :], itf[:, 0:NE], float(REG), None, ALU.mult))
            gp.wait_ge(s["c"], 16 * 7)
            gp.sem_inc(s["scd"], 1)
            with gp.Fori(0, B) as b:
                for i in range(NS):
                    if i < QT:
                        gp.wait_ge(s["x2"], b * QT + i + 1 + CR)
                        gp.wait_ge(s["x3"], b * QT + max(i - 3, 0) + CR)
                        gp.tensor_tensor(x2b[:, i % 4, :], x2[:, i % 2, :], bo[:, :], ALU.add).then_inc(s["x2b"], 1)
                    if 0 <= i - 1 < QT:
                        j = i - 1
                        gp.wait_ge(s["hrs"], b * QT + j + 1)
                        gp.wait_ge(s["T"], b * 3 * QT + (turns.index(("q", j - 2)) + 1 if j >= 2 else 0) + CR)
                        gp.tensor_tensor(qn[:, j % 2, :].rearrange("p (h j) -> p h j", h=XH),
                                         qc[:, j % 2, :].rearrange("p (h j) -> p h j", h=XH),
                                         hs3[:, j % 2, :].unsqueeze(2).broadcast_to([P, XH, XD]),
                                         ALU.mult).then_inc(s["qn"], 1)
                    if 0 <= i - 4 < QT:
                        j = i - 4
                        wait_alone(gp, s["pos"], b * QT + j + 1 + CR, s["any"])
                        for k in range(2):
                            gp.indirect_dma_start(dram["hs"][:, :],
                                                  bass.IndirectOffsetOnAxis(ap=pi[:, j, k:k + 1], axis=0),
                                                  hn[:, j, :], None).then_inc(s[f"sc{j % 4}"], 16)
                for k in range(4):
                    gp.wait_ge(s[f"sc{k}"], 32 * QT // 4 * (b + 1))
                gp.sem_inc(s["scd"], 1)

        @block.tensor
        def _(pe):
            pe.sem_inc(s["mwp"], CR)
            pe.sem_inc(s["T"], CR)
            pe.wait_ge(s["w"], 32)
            pe.wait_ge(s["c"], 16 * 7)
            pe.wait_ge(s["pool"], 11)

            def parts(out, lhs, rhs, k, n):
                pe.matmul(out, lhs(0), rhs(0), start=k == 0, stop=False)
                pe.matmul(out, lhs(0), rhs(1), start=False, stop=False)
                return pe.matmul(out, lhs(1), rhs(0), start=False, stop=k == n - 1)

            with pe.Fori(0, B) as b:
                pe.wait_ge(s["bd"], 64 * (b + 1))
                for q in range(4):
                    pe.wait_ge(s["mwl"], 4 * b + q + CR)
                    if q == 0:
                        pe.wait_ge(s["pos"], QT * b + CR)
                    pe.matmul(pW[:, :], bd[:, q, :], wo[:, q, :], start=True, stop=True).then_inc(s["mwp"], 1)
                for i in range(NS):
                    def turn(kind, j, src, ready):
                        pe.wait_ge(s[ready[0]], b * QT + j + 1 + ready[1])
                        wait_turn(pe, b, kind, j)
                        for e in range(ET):
                            mm = pe.transpose(pT[slot(kind, j)][:, e * P:(e + 1) * P],
                                              src[:, e * P:(e + 1) * P], ident[:, :])
                        mm.then_inc(s["T"], 1)

                    if 0 <= i - 1 < QT:
                        turn("n", i - 1, n2[:, (i - 1) % 2, :], ("n2", 0))
                    if 0 <= i - 2 < QT:
                        turn("q", i - 2, qn[:, (i - 2) % 2, :], ("qn", 0))
                    if 0 <= i - 3 < QT:
                        turn("h", i - 3, hn[:, i - 3, :], ("hn", 0))
                    if 0 <= i - 4 < QT:
                        j = i - 4
                        pe.wait_ge(s["ms"], b * QT + j + 1)
                        pe.wait_ge(s["pos"], b * QT + j + CR)
                        if j == 0:
                            pe.wait_ge(s["mwl"], 4 * (b + 1) + CR)
                        pe.matmul(pW[:, 0:NE], tri[:, :], msum[:, j % 2, :], start=True, stop=False)
                        pe.matmul(pW[:, 0:NE], ones[:, :], cum[:, :], start=False, stop=True
                                  ).then_inc(s["rank"], 1)
                    if i < QT:
                        pe.wait_ge(s["alo"], b * QT + i + 1 + CR)
                        pe.wait_ge(s["x2"], b * QT + i - 1 + CR)
                        for f in range(8):
                            mm = parts(pA[i % 2][:, :], lambda a: ap[:, i % 2, a, f, :],
                                       lambda a: ww[:, a, f * D:(f + 1) * D], f, 8)
                        mm.then_inc(s["A"], 1)
                    if 0 <= i - 1 < QT:
                        j = i - 1
                        pe.wait_ge(s["nlo"], b * QT + j + 1 + CR)
                        pe.wait_ge(s["qc"], b * QT + j + CR)
                        for e in range(ET):
                            mm = parts(pQ[:, :], lambda a: nT[:, j % 2, a, e, :],
                                       lambda a: ww[:, a, (8 + e) * D:(9 + e) * D], e, ET)
                        mm.then_inc(s["Q"], 1)
                    if 0 <= i - 2 < QT:
                        j = i - 2
                        pe.wait_ge(s["qlo"], b * QT + j + 1)
                        pe.wait_ge(s["x3"], b * QT + j + CR)
                        if j == 0:
                            pe.wait_ge(s["mwl"], 4 * (b + 1) + CR)
                        for e in range(ET):
                            mm = parts(pM[:, :], lambda a: qT[:, j % 2, a, e, :],
                                       lambda a: mw[:, a, e, :], e, ET)
                        mm.then_inc(s["M"], 1)
                    if 0 <= i - 3 < QT:
                        j = i - 3
                        pe.wait_ge(s["hT"], b * QT + j + 1 + CR)
                        pe.wait_ge(s["rt"], b * QT + j + CR)
                        for e in range(ET):
                            mm = pe.matmul(pR[:, 0:NE], hT[:, j % 2, e, :], rw[:, e, :],
                                           start=e == 0, stop=e == ET - 1)
                        mm.then_inc(s["R"], 1)
            pe.wait_ge(s["pos"], NT + CR)
            pe.matmul(pW[:, 0:NE], ones[:, :], cum[:, :], start=True, stop=True).then_inc(s["tot"], 1)

        @block.scalar
        def _(act):
            act.sem_inc(s["qf"], CR)
            act.sem_inc(s["hT"], CR)
            act.sem_inc(s["ahi"], CR)
            act.wait_ge(s["c"], 16 * 7)
            act.wait_ge(s["pool"], 11)
            with act.Fori(0, B) as b:
                for q in range(4):
                    act.wait_ge(s["mwp"], 4 * b + q + 1 + CR)
                    if q == 0:
                        act.wait_ge(s["x3"], QT * b + CR)
                    act.activation(mw[:, 0, q, :], pW[:, :], ACT.Copy).then_inc(s["mwh"], 1)

                def att_high(i):
                    act.wait_ge(s["an"], b * QT + i + 1)
                    act.wait_ge(s["x2"], b * QT + i - 1 + CR)
                    act.activation(ap[:, i % 2, 0, :, :], att[:, i % 2, :, :], ACT.Copy).then_inc(s["ahi"], 1)

                def turned(kind, j):
                    return b * 3 * QT + turns.index((kind, j)) + 1 + CR

                att_high(0)
                for i in range(NS):
                    if 0 <= i - 1 < QT:
                        j = i - 1
                        act.wait_ge(s["T"], turned("n", j))
                        act.wait_ge(s["qc"], b * QT + j - 1 + CR)
                        act.activation(nT[:, j % 2, 0, :, :],
                                       pT[slot("n", j)][:, :].rearrange("p (e t) -> p e t", e=ET),
                                       ACT.Copy).then_inc(s["nhi"], 1)
                    if 0 <= i - 2 < QT:
                        j = i - 2
                        act.wait_ge(s["T"], turned("q", j))
                        if j:
                            act.wait_ge(s["qlo"], b * QT + j)
                        act.activation(qf[:, :], pT[slot("q", j)][:, :], ACT.Identity, bias=bq[:, 0:1],
                                       scale=gq[:, 0:1]).then_inc(s["qf"], 1)
                        act.wait_ge(s["x3"], b * QT + j - 1 + CR)
                        act.wait_ge(s["qf"], b * QT + j + 1 + CR)
                        act.activation(qT[:, j % 2, 0, :, :], qf[:, :].rearrange("p (e t) -> p e t", e=ET),
                                       ACT.Copy).then_inc(s["qhi"], 1)
                    if 0 <= i - 3 < QT:
                        j = i - 3
                        act.wait_ge(s["T"], turned("h", j))
                        act.wait_ge(s["rt"], b * QT + j - 1 + CR)
                        act.activation(hT[:, j % 2, :, :],
                                       pT[slot("h", j)][:, :].rearrange("p (e t) -> p e t", e=ET),
                                       ACT.Copy).then_inc(s["hT"], 1)
                    if i + 1 < QT:
                        att_high(i + 1)
                    if i < QT:
                        act.wait_ge(s["mv"], lnorm(b, i, 0))
                        act.activation(sd[:, 0:1], mv[:, 0, 1:2], ACT.Sqrt, bias=eps[:, 0:1]).then_inc(s["sd"], 1)
                    if 0 <= i - 1 < QT:
                        j = i - 1
                        act.wait_ge(s["qc"], b * QT + j + 1 + CR)
                        act.activation(sq[:, :], qc[:, j % 2, :], ACT.Square).then_inc(s["sq"], 1)
                        act.wait_ge(s["hvar"], 2 * (b * QT + j + 1))
                        act.activation(hs2[:, j % 2, :], hs1[:, j % 2, :], ACT.Sqrt, bias=eps[:, 0:1],
                                       scale=1.0 / XD).then_inc(s["hsd"], 1)
                    if 0 <= i - 2 < QT:
                        act.wait_ge(s["mv"], lnorm(b, i, 1))
                        act.activation(sd[:, 1:2], mv[:, 1, 1:2], ACT.Sqrt, bias=eps[:, 0:1]).then_inc(s["sd"], 1)
            act.wait_ge(s["e"], 1)
            act.activation(e2[:, :], e2[:, :], ACT.Exp).then_inc(s["e"], 1)

        @block.vector
        def _(dve):
            for k in ("x2", "x3", "alo", "nlo", "qc", "rt", "pos", "mwl"):
                dve.sem_inc(s[k], CR)
            dve.sem_inc(s["st30"], 16)
            dve.sem_inc(s["st31"], 16)
            dve.wait_ge(s["pool"], 11)
            dve.wait_ge(s["c"], 16 * 7)
            with dve.Fori(0, B) as b:
                for q in range(4):
                    dve.wait_ge(s["mwh"], 4 * b + q + 1)
                    dve.tensor_tensor(mw[:, 1, q, :], pW[:, :], mw[:, 0, q, :].bitcast(F32),
                                      ALU.subtract).then_inc(s["mwl"], 1)

                def att_scale(i):
                    dve.wait_ge(s[f"attl{i % 2}"], 48 * (b * QT // 2 + i // 2 + 1))
                    dve.tensor_tensor(att[:, i % 2, :, :], att[:, i % 2, :, :], rb[:, i % 2, :, :],
                                      ALU.mult).then_inc(s["an"], 1)

                def att_low(i):
                    dve.wait_ge(s["ahi"], b * QT + i + 1 + CR)
                    dve.tensor_tensor(ap[:, i % 2, 1, :, :], att[:, i % 2, :, :],
                                      ap[:, i % 2, 0, :, :].bitcast(F32), ALU.subtract).then_inc(s["alo"], 1)

                def norm(i, k, src, dst, sem):
                    c = lnorm(b, i, k)
                    dve.bn_stats(st[:, k, :], src).then_inc(s["bn"], 1)
                    wait_alone(dve, s["bn"], c, s["any"])
                    dve.bn_aggr(mv[:, k, :], st[:, k, :]).then_inc(s["mv"], 1)
                    dve.wait_ge(s["sd"], c)
                    dve.reciprocal(rs[:, k:k + 1], sd[:, k:k + 1]).then_inc(s["rs"], 1)
                    dve.wait_ge(s["rs"], c)
                    dve.tensor_scalar(dst, src, mv[:, k, 0:1], rs[:, k:k + 1], ALU.subtract,
                                      ALU.mult).then_inc(s[sem], 1)

                att_scale(0)
                att_low(0)
                for i in range(NS):
                    if 0 <= i - 1 < QT:
                        j = i - 1
                        dve.wait_ge(s["nhi"], b * QT + j + 1)
                        dve.tensor_tensor(nT[:, j % 2, 1, :, :],
                                          pT[slot("n", j)][:, :].rearrange("p (e t) -> p e t", e=ET),
                                          nT[:, j % 2, 0, :, :].bitcast(F32), ALU.subtract).then_inc(s["nlo"], 1)
                    if 0 <= i - 2 < QT:
                        j = i - 2
                        dve.wait_ge(s["qhi"], b * QT + j + 1)
                        dve.tensor_tensor(qT[:, j % 2, 1, :, :], qf[:, :].rearrange("p (e t) -> p e t", e=ET),
                                          qT[:, j % 2, 0, :, :].bitcast(F32), ALU.subtract).then_inc(s["qlo"], 1)
                    if i + 1 < QT:
                        att_scale(i + 1)
                        att_low(i + 1)
                    if i < QT:
                        dve.wait_ge(s["A"], b * QT + i + 1)
                        dve.wait_ge(s[f"xl{i % 2}"], 16 * (b * QT // 2 + i // 2 + 1))
                        if i >= 2:
                            dve.wait_ge(s["x2b"], b * QT + i - 1)
                        dve.tensor_tensor(x2[:, i % 2, :], pA[i % 2][:, :], x[:, i % 2, :],
                                          ALU.add).then_inc(s["x2"], 1)
                        dve.wait_ge(s["x2"], b * QT + i + 1 + CR)
                        norm(i, 0, x2[:, i % 2, :], n2[:, i % 2, :], "n2")
                    if 0 <= i - 1 < QT:
                        j = i - 1
                        c = b * QT + j + 1
                        q3 = pQ[:, :].rearrange("p (h j) -> p h j", h=XH)
                        dve.wait_ge(s["Q"], c)
                        dve.tensor_reduce(hs1[:, j % 2, :], q3, AXX, ALU.add).then_inc(s["hvar"], 1)
                        dve.wait_ge(s["hvar"], 2 * c - 1)
                        if j >= 2:
                            dve.wait_ge(s["qn"], c - 2)
                        dve.tensor_scalar(hs3[:, j % 2, :], hs1[:, j % 2, :], 1.0 / XD, None,
                                          ALU.mult).then_inc(s["hmean"], 1)
                        dve.wait_ge(s["hmean"], c)
                        dve.tensor_tensor(qc[:, j % 2, :].rearrange("p (h j) -> p h j", h=XH), q3,
                                          hs3[:, j % 2, :].unsqueeze(2).broadcast_to([P, XH, XD]),
                                          ALU.subtract).then_inc(s["qc"], 1)
                        dve.wait_ge(s["sq"], c)
                        dve.tensor_reduce(hs1[:, j % 2, :], sq[:, :].rearrange("p (h j) -> p h j", h=XH), AXX,
                                          ALU.add).then_inc(s["hvar"], 1)
                        dve.wait_ge(s["hsd"], c)
                        dve.reciprocal(hs3[:, j % 2, :], hs2[:, j % 2, :]).then_inc(s["hrs"], 1)
                    if 0 <= i - 2 < QT:
                        j = i - 2
                        c = b * QT + j + 1
                        dve.wait_ge(s["M"], c)
                        dve.wait_ge(s["x2b"], c)
                        dve.wait_ge(s[f"st3{j % 2}"], 16 * (b * QT // 2 + j // 2 + 1))
                        dve.tensor_tensor(x3[:, j % 2, :], pM[:, :], x2b[:, j % 4, :], ALU.add).then_inc(s["x3"], 1)
                        dve.wait_ge(s["x3"], c + CR)
                        if j == 0:
                            dve.wait_ge(s["scd"], b + 1)
                        norm(i, 1, x3[:, j % 2, :], hn[:, j, :], "hn")
                    if 0 <= i - 3 < QT:
                        j = i - 3
                        c = b * QT + j + 1
                        dve.wait_ge(s["R"], c)
                        dve.tensor_tensor(lg[:, :], pR[:, 0:NE], rbias[:, :], ALU.add).then_inc(s["rt"], 1)
                        wait_alone(dve, s["rt"], c + CR, s["any"])
                        r = (b * QT + j) * 4
                        dve.max(top8[:, j, :], lg[:, :]).then_inc(s["dc"], 1)
                        wait_alone(dve, s["dc"], r + 1, s["any"])
                        dve.max_index(ix8[:, :], top8[:, j, :], lg[:, :]).then_inc(s["dc"], 1)
                        dve.wait_ge(s["dc"], r + 2)
                        dve.tensor_copy(idx[:, j % 2, :], ix8[:, :]).then_inc(s["dc"], 1)
                        dve.wait_ge(s["dc"], r + 3)
                        dve.tensor_scalar(m1[:, :], iota8[:, :], idx[:, j % 2, 0:1], None,
                                          ALU.is_equal).then_inc(s["dc"], 1)
                        dve.wait_ge(s["dc"], r + 4)
                        dve.scalar_tensor_tensor(out=msum[:, j % 2, :], in0=iota8[:, :], scalar=idx[:, j % 2, 1:2],
                                                 in1=m1[:, :], op0=ALU.is_equal, op1=ALU.add
                                                 ).then_inc(s["ms"], 1)
                    if 0 <= i - 4 < QT:
                        j = i - 4
                        c = b * QT + j + 1
                        r = (b * QT + j) * 4
                        dve.wait_ge(s["rank"], c)
                        dve.tensor_tensor(pr[:, :], pW[:, 0:NE], base[:, :], ALU.add).then_inc(s["cnt"], 1)
                        dve.tensor_tensor(cum[:, :], cum[:, :], msum[:, j % 2, :], ALU.add).then_inc(s["cumd"], 1)
                        dve.wait_ge(s["cnt"], r + 1)
                        for k in range(2):
                            if k:
                                dve.wait_ge(s["cnt"], r + 2)
                            dve.scalar_tensor_tensor(out=junk[:, :], in0=iota8[:, :], scalar=idx[:, j % 2, k:k + 1],
                                                     in1=pr[:, :], op0=ALU.is_equal, op1=ALU.mult,
                                                     accum_out=pf[:, j % 2, k:k + 1]).then_inc(s["cnt"], 1)
                        dve.wait_ge(s["cnt"], r + 3)
                        dve.wait_ge(s["cumd"], c)
                        dve.tensor_copy(pi[:, j, :], pf[:, j % 2, :]).then_inc(s["pos"], 1)
                        dve.sem_inc(s["cnt"], 1)
                wait_alone(dve, s["pos"], (b + 1) * QT + CR, s["any"])
                dve.tensor_copy(route["pos"][:, bass.ds(b * QT, QT), :], pi[:, :, :]).then_inc(s["keep"], 1)
                dve.tensor_copy(route["top"][:, bass.ds(b * QT, QT), :], top8[:, :, 0:2]).then_inc(s["keep"], 1)
                dve.wait_ge(s["keep"], 2 * b + 2)
            ch = Chain(dve, s["tb"])
            dve.tensor_tensor(e2[:, :], route["top"][:, :, 1], route["top"][:, :, 0], ALU.subtract).then_inc(s["e"], 1)
            dve.wait_ge(s["e"], 2)
            ch.step(dve.tensor_scalar(route["w"][:, :, 0], e2[:, :], 1.0, None, ALU.add))
            ch.step(dve.reciprocal(route["w"][:, :, 0], route["w"][:, :, 0]))
            ch.step(dve.tensor_tensor(route["w"][:, :, 1], e2[:, :], route["w"][:, :, 0], ALU.mult))
            dve.wait_ge(s["tot"], 1)
            ch.step(dve.tensor_copy(cnt[:, :], pW[:, 0:NE]))
            ch.step(dve.tensor_scalar(nb[:, :], cnt[:, :], 0.0, None, ALU.is_gt))
            for m in range(1, TOK // BLK):
                ch.step(dve.scalar_tensor_tensor(out=nb[:, :], in0=cnt[:, :], scalar=float(m * BLK), in1=nb[:, :],
                                                 op0=ALU.is_gt, op1=ALU.add))
            ch.step(dve.tensor_copy(end[:, 0:1], nb[:, 0:1]))
            for e in range(1, NE):
                ch.step(dve.tensor_tensor(end[:, e:e + 1], end[:, e - 1:e], nb[:, e:e + 1], ALU.add))
            E, before, t0, t1 = (tb[:, k, :] for k in range(4))
            ch.do(dve.memset(tb[:, 0:2, :], 0.0))
            ch.sync()
            for e in range(NE):
                ch.step(dve.tensor_scalar(t0, itf[:, :], end[:, e:e + 1], None, ALU.is_ge))
                ch.step(dve.tensor_tensor(E, E, t0, ALU.add))
                ch.step(dve.scalar_tensor_tensor(out=before, in0=t0, scalar=nb[:, e:e + 1], in1=before,
                                                 op0=ALU.mult, op1=ALU.add))
            ch.step(dve.tensor_tensor(before, itf[:, :], before, ALU.subtract))
            ch.step(dve.tensor_scalar(before, before, float(BLK), None, ALU.mult))
            ch.step(dve.tensor_scalar(t1, E, NE - 0.5, None, ALU.is_lt))
            ch.step(dve.tensor_tensor(before, before, t1, ALU.mult))
            ch.step(dve.tensor_scalar(E, E, NE - 1.0, None, ALU.min))
            ch.step(dve.tensor_copy(route["tab"][:, 0, :], E))
            ch.step(dve.scalar_tensor_tensor(out=t0, in0=E, scalar=float(REG), in1=before,
                                             op0=ALU.mult, op1=ALU.add))
            ch.step(dve.tensor_copy(route["tab"][:, 1, :], t0))
            ch.step(dve.tensor_tensor(nb[:, :], end[:, :], nb[:, :], ALU.subtract))
            ch.step(dve.scalar_tensor_tensor(out=nb[:, :], in0=nb[:, :], scalar=float(BLK), in1=base[:, :],
                                             op0=ALU.mult, op1=ALU.subtract))
            posf, yrow, mask = (tp[:, k, :] for k in range(3))
            ch.step(dve.tensor_copy(posf, route["pos"][:, :, :].rearrange("p t k -> p (t k)")))
            ch.step(dve.tensor_copy(yrow, posf))
            for e in range(NE):
                ch.step(dve.tensor_scalar(mask, posf, float(e * REG), None, ALU.is_ge))
                ch.step(dve.scalar_tensor_tensor(out=mask, in0=posf, scalar=float((e + 1) * REG), in1=mask,
                                                 op0=ALU.is_lt, op1=ALU.mult))
                ch.step(dve.scalar_tensor_tensor(out=yrow, in0=mask, scalar=nb[:, e:e + 1], in1=yrow,
                                                 op0=ALU.mult, op1=ALU.add))
            ch.step(dve.tensor_copy(route["pos"][:, :, :].rearrange("p t k -> p (t k)"), yrow))
            ch.step(dve.tensor_tensor(cnt[:, :], cnt[:, :], base[:, :], ALU.add))
            dve.tensor_copy(route["tab"][:, 3, 0:NE], cnt[:, :]).then_inc(s["fin"], 1)


def expert_phase(nc, io, dram, route):
    with Room(nc, "e_") as rm:
        WM = ET * D
        RT = BLK // P
        raw = rm.sb("raw", [P, 3, WM])
        w = rm.sb("w", [P, 3, 2, WM], F32R)
        rows = rm.sb("rows", [P, RT, D])
        hT = rm.sb("hT", [P, 2, ET, BLK], F32R)
        sil = rm.sb("sil", [P, 2, BLK])
        a32 = rm.sb("a32", [P, 2, BLK])
        aT = rm.sb("aT", [P, 2, ET, BLK], F32R)
        y = rm.sb("y", [P, RT, D])
        ident = rm.sb("ident", [P, P])
        pT, pG, pU, pY = ([rm.ps(f"{n}{i}", [P, 512]) for i in range(2)] for n in "TGUY")
        names = "any id rows rawg rawu rawd whi wlo T thi tlo G U sil mul ahi alo Y y st".split()
        s = {k: rm.sem(k) for k in names}
        block = rm.ctx.enter_context(nc.Block())

        @block.sync
        def _(sp):
            def entry(kind, j, top):
                return sp.value_load(route["tab"][0:1, kind, bass.ds(j, 1)], min_val=0, max_val=top)

            def load_rows(j):
                r = entry(1, j, NE * REG - BLK)
                sp.dma_start(rows[:, :, :], dram["hs"][bass.ds(r, BLK), :].rearrange("(t p) d -> p t d", p=P)
                             ).then_inc(s["rows"], 16)

            def load_weight(k, e):
                sp.dma_start(raw[:, k, :], io["we"][bass.ds(e, 1), k].rearrange("o p n -> (o p) n")
                             ).then_inc(s[("rawg", "rawu", "rawd")[k]], 16)

            sp.dma_start(ident[:, :], io["ident"]).then_inc(s["id"], 16)
            load_rows(0)
            e0 = entry(0, 0, NE - 1)
            for k in range(3):
                load_weight(k, e0)
            with sp.Fori(0, NBLK) as j:
                e = entry(0, j + 1, NE - 1)
                wait_alone(sp, s["tlo"], 4 * j + 4 + 2, s["any"])
                load_rows(j + 1)
                for k in range(2):
                    wait_alone(sp, s["wlo"], 3 * j + k + 1, s["any"])
                    load_weight(k, e)
                wait_alone(sp, s["wlo"], 3 * j + 3, s["any"])
                load_weight(2, e)
                wait_alone(sp, s["y"], 4 * j + 4 + 2, s["any"])
                sp.dma_start(dram["ys"][bass.ds(j * BLK, BLK), :].rearrange("(t p) d -> p t d", p=P),
                             y[:, :, :]).then_inc(s["st"], 16)
            for k in ("rows", "rawg", "rawu", "rawd", "st"):
                sp.wait_ge(s[k], 16 * (NBLK + 1))

        def split(eng, j, k, part):
            if part == 0:
                eng.wait_ge(s[("rawg", "rawu", "rawd")[k]], 16 * (j + 1))
                eng.activation(w[:, k, 0, :], raw[:, k, :], ACT.Copy).then_inc(s["whi"], 1)
            else:
                eng.wait_ge(s["whi"], 3 * j + k + 1)
                eng.tensor_tensor(w[:, k, 1, :], raw[:, k, :], w[:, k, 0, :].bitcast(F32),
                                  ALU.subtract).then_inc(s["wlo"], 1)

        @block.tensor
        def _(pe):
            def parts(out, lhs, rhs, k):
                pe.matmul(out, lhs(0), rhs(0), start=k == 0, stop=False)
                pe.matmul(out, lhs(0), rhs(1), start=False, stop=False)
                return pe.matmul(out, lhs(1), rhs(0), start=False, stop=k == ET - 1)

            def turn(j):
                pe.wait_ge(s["rows"], 16 * (j + 1))
                for e in range(ET):
                    pe.wait_ge(s["tlo"], 4 * j + e - 1 + 2)
                    for t in range(RT):
                        mm = pe.transpose(pT[e % 2][:, t * P:(t + 1) * P], rows[:, t, e * P:(e + 1) * P],
                                          ident[:, :])
                    mm.then_inc(s["T"], 1)

            pe.wait_ge(s["id"], 16)
            turn(0)
            with pe.Fori(0, NBLK) as j:
                pe.wait_ge(s["wlo"], 3 * j + 2)
                pe.wait_ge(s["tlo"], 4 * j + 4 + 2)
                for f in range(ET):
                    pe.wait_ge(s["mul"], 4 * j + f - 1 + 2)
                    for k, out, sem in ((0, pG, "G"), (1, pU, "U")):
                        for e in range(ET):
                            mm = parts(out[f % 2][:, :],
                                       lambda a: w[:, k, a, e * D + f * P:e * D + (f + 1) * P],
                                       lambda a: hT[:, a, e, :], e)
                        mm.then_inc(s[sem], 1)
                turn(j + 1)
                pe.wait_ge(s["alo"], 4 * j + 4)
                pe.wait_ge(s["wlo"], 3 * j + 3)
                for t in range(RT):
                    pe.wait_ge(s["y"], 4 * j + t - 1 + 2)
                    for f in range(ET):
                        mm = parts(pY[t % 2][:, :], lambda a: aT[:, a, f, t * P:(t + 1) * P],
                                   lambda a: w[:, 2, a, f * D:(f + 1) * D], f)
                    mm.then_inc(s["Y"], 1)

        @block.scalar
        def _(act):
            act.sem_inc(s["y"], 2)

            def turn_high(j):
                for e in range(ET):
                    act.wait_ge(s["T"], 4 * j + e + 1)
                    act.activation(hT[:, 0, e, :], pT[e % 2][:, :], ACT.Copy).then_inc(s["thi"], 1)

            turn_high(0)
            split(act, 0, 0, 0)
            split(act, 0, 1, 0)
            with act.Fori(0, NBLK) as j:
                act.wait_ge(s["Y"], 4 * j + 1)
                split(act, j, 2, 0)
                for f in range(ET):
                    act.wait_ge(s["G"], 4 * j + f + 1)
                    act.wait_ge(s["mul"], 4 * j + f - 1 + 2)
                    act.activation(sil[:, f % 2, :], pG[f % 2][:, :], ACT.Silu).then_inc(s["sil"], 1)
                    act.wait_ge(s["mul"], 4 * j + f + 1 + 2)
                    act.activation(aT[:, 0, f, :], a32[:, f % 2, :], ACT.Copy).then_inc(s["ahi"], 1)
                turn_high(j + 1)
                act.wait_ge(s["U"], 4 * j + 4)
                split(act, j + 1, 0, 0)
                split(act, j + 1, 1, 0)
                act.wait_ge(s["st"], 16 * j + 16)
                for t in range(RT):
                    act.wait_ge(s["Y"], 4 * j + t + 1 + 1)
                    act.activation(y[:, t, :], pY[t % 2][:, :], ACT.Copy).then_inc(s["y"], 1)

        @block.vector
        def _(dve):
            dve.sem_inc(s["tlo"], 2)
            dve.sem_inc(s["mul"], 2)
            dve.sem_inc(s["st"], 16)
            dve.sem_inc(s["Y"], 1)

            def turn_low(j):
                for e in range(ET):
                    dve.wait_ge(s["thi"], 4 * j + e + 1)
                    dve.tensor_tensor(hT[:, 1, e, :], pT[e % 2][:, :], hT[:, 0, e, :].bitcast(F32),
                                      ALU.subtract).then_inc(s["tlo"], 1)

            turn_low(0)
            split(dve, 0, 0, 1)
            split(dve, 0, 1, 1)
            with dve.Fori(0, NBLK) as j:
                split(dve, j, 2, 1)
                for f in range(ET):
                    dve.wait_ge(s["U"], 4 * j + f + 1)
                    dve.wait_ge(s["sil"], 4 * j + f + 1)
                    dve.tensor_tensor(a32[:, f % 2, :], pU[f % 2][:, :], sil[:, f % 2, :],
                                      ALU.mult).then_inc(s["mul"], 1)
                    dve.wait_ge(s["ahi"], 4 * j + f + 1)
                    dve.tensor_tensor(aT[:, 1, f, :], a32[:, f % 2, :], aT[:, 0, f, :].bitcast(F32),
                                      ALU.subtract).then_inc(s["alo"], 1)
                turn_low(j + 1)
                split(dve, j + 1, 0, 1)
                split(dve, j + 1, 1, 1)


def combine_phase(nc, io, dram, route):
    R = 4
    with Room(nc, "o_") as rm:
        x = rm.sb("x", [P, R, D])
        y = rm.sb("y", [P, R, 2, D])
        o = rm.sb("o", [P, R, D])
        pi = rm.sb("pi", [P, R, 2], I32)
        w = rm.sb("w", [P, R, 2])
        s_x, s_y, s_o = ([rm.sem(f"{n}{i}") for i in range(R)] for n in "xyo")
        s_any = rm.sem("any")
        s_pi = rm.sem("pi")
        s_w = rm.sem("w")
        s_add = rm.sem("add")
        block = rm.ctx.enter_context(nc.Block())
        N = NT // R

        @block.sync
        def _(sp):
            with sp.Fori(0, N) as i:
                for k in range(R):
                    wait_alone(sp, s_add, 2 * (i * R + k) + 2, s_any)
                    sp.dma_start(x[:, k, :], dram["x3"][bass.ds((i * R + k) * P, P), :]).then_inc(s_x[k], 16)
            for k in range(R):
                sp.wait_ge(s_x[k], 16 * N)

        @block.gpsimd
        def _(gp):
            with gp.Fori(0, N) as i:
                for k in range(R):
                    wait_alone(gp, s_pi, i * R + k + 1, s_any)
                    wait_alone(gp, s_add, 2 * (i * R + k) + 2, s_any)
                    for a in range(2):
                        gp.indirect_dma_start(y[:, k, a, :], None, dram["ys"][:, :],
                                              bass.IndirectOffsetOnAxis(ap=pi[:, k, a:a + 1], axis=0)
                                              ).then_inc(s_y[k], 16)
            for k in range(R):
                gp.wait_ge(s_y[k], 32 * N)

        @block.vector
        def _(dve):
            dve.sem_inc(s_add, 2 * R)
            for k in range(R):
                dve.sem_inc(s_o[k], 16)
            with dve.Fori(0, N) as i:
                for k in range(R):
                    t = i * R + k
                    wait_alone(dve, s_add, 2 * t + 2, s_any)
                    dve.tensor_copy(pi[:, k, :].unsqueeze(1), route["pos"][:, bass.ds(t, 1), :]).then_inc(s_pi, 1)
                    dve.tensor_copy(w[:, k, :].unsqueeze(1), route["w"][:, bass.ds(t, 1), :]).then_inc(s_w, 1)
                for k in range(R):
                    t = i * R + k
                    dve.wait_ge(s_w, t + 1)
                    dve.wait_ge(s_x[k], 16 * i + 16)
                    dve.wait_ge(s_y[k], 32 * i + 32)
                    dve.wait_ge(s_o[k], 16 * i + 16)
                    dve.scalar_tensor_tensor(out=x[:, k, :], in0=y[:, k, 0, :], scalar=w[:, k, 0:1],
                                             in1=x[:, k, :], op0=ALU.mult, op1=ALU.add).then_inc(s_add, 1)
                    dve.wait_ge(s_add, 2 * t + 1 + 2 * R)
                    dve.scalar_tensor_tensor(out=o[:, k, :], in0=y[:, k, 1, :], scalar=w[:, k, 1:2],
                                             in1=x[:, k, :], op0=ALU.mult, op1=ALU.add).then_inc(s_add, 1)

        @block.scalar
        def _(act):
            with act.Fori(0, N) as i:
                for k in range(R):
                    t = i * R + k
                    wait_alone(act, s_add, 2 * t + 2 + 2 * R, s_any)
                    act.dma_start(io["out"][bass.ds(t * P, P), :], o[:, k, :]).then_inc(s_o[k], 16)
            for k in range(R):
                act.wait_ge(s_o[k], 16 * N + 16)


def kernel(**inputs):
    import concourse.bacc as bacc
    from concourse.bass_utils import run_bass_kernel_spmd as run

    def rows(w):
        return w.reshape(-1, P, w.shape[1]).transpose(1, 0, 2).reshape(P, -1)

    a = {k: np.ascontiguousarray(v) for k, v in inputs.items()}
    q, k, v = np.split(a["L0_attn_W_qkv"], 3, axis=1)

    def halves(w, g):
        w = w.reshape(D, H, HD // 2, 2)[:, g * GH:(g + 1) * GH]
        return w.transpose(0, 3, 1, 2).reshape(D, 2 * P)

    wts = [rows(np.concatenate([halves(q, g), halves(k, g), v[:, g * GH * HD:(g + 1) * GH * HD]], axis=1))
           for g in range(G)]
    tail = np.concatenate([rows(a["L0_attn_W_out"]), rows(a["L0_xattn_Wq"].T)], axis=1)
    wts += [tail[:, :WCOLS], tail[:, WCOLS:]]
    freqs = 1.0 / np.float32(10000.0) ** (np.arange(0, HD, 2, dtype=np.float32) / np.float32(HD))
    angles = (np.arange(T, dtype=np.float32)[:, None] * freqs.astype(np.float32)[None, :]).astype(np.float32)
    rot = np.tile(angles.T, (GH, 1))
    arrays = {
        "x": a["x"].reshape(TOK, D), "ctx": a["ctx_1024"].reshape(B * TC, D), "wts": np.stack(wts),
        "wkT": a["L0_xattn_Wk"].T, "wvT": a["L0_xattn_Wv"].T,
        "wgT": np.concatenate([a["L0_xattn_Wbeta"], a["L0_xattn_Walpha"]], axis=0).T,
        "gbias": np.concatenate([a["L0_xattn_bbeta"], a["L0_xattn_balpha"]]),
        "gk": a["L0_xattn_gk"], "bk": a["L0_xattn_bk"],
        "woT": a["L0_xattn_Wo"].T, "bo": a["L0_xattn_bo"],
        "gq": np.tile(a["L0_xattn_gq"], P // XD)[:, None], "bq": np.tile(a["L0_xattn_bq"], P // XD)[:, None],
        "rw": a["L0_ffn_router_w"], "rb": a["L0_ffn_router_b"],
        "we": np.stack([np.stack([rows(a[n][e]) for n in ("L0_ffn_we_gate", "L0_ffn_we_up", "L0_ffn_we_down")])
                        for e in range(NE)]),
        "cos": np.cos(rot), "sin": np.sin(rot), "ident": np.eye(P, dtype=np.float32),
    }
    arrays = {"in_" + n: np.ascontiguousarray(x) for n, x in arrays.items()}
    nc = bacc.Bacc("TRN2", target_bir_lowering=False, num_devices=1)
    io = {n[3:]: nc.dram_tensor(n, x.shape, mybir.dt.from_np(x.dtype), kind="ExternalInput").ap()
          for n, x in arrays.items()}
    io["out"] = nc.dram_tensor("out", (TOK, D), F32, kind="ExternalOutput").ap()
    program(nc, io)
    r = run(nc, [arrays], core_ids=[0])
    return r.results[0]["out"].reshape(B, T, D)
```

```python
from contextlib import ExitStack

import concourse.bass as bass
from concourse import mybir
import numpy as np

F32 = mybir.dt.float32
F32R = mybir.dt.float32r
BF16 = mybir.dt.bfloat16
I32 = mybir.dt.int32
U32 = mybir.dt.uint32
ALU = mybir.AluOpType
ACT = mybir.ActivationFunctionType
AXX = mybir.AxisListType.X

P = 128
B, T, D = 4, 1024, 512
TOK = B * T
NT = TOK // P
ET = D // P
H, HD = 16, 64
SCALE = HD ** -0.5
assert SCALE == 0.125
GH = 4
G = H // GH
QT = T // P
GW = 3 * GH * HD
WCOLS = ET * GW
XH, XD = 16, 32
TC = 64
CT = B * TC // P
NE = 8
BLK = 512
REG = TOK + BLK
NBLK = (2 * TOK) // BLK + NE - 1
EPS = 1e-5
EPS_NORM = 1e-12
CREDIT = 2
MASKED = -1e30


def program(nc, io):
    dram = {}

    def scratch(name, shape, dt):
        dram[name] = nc.dram_tensor("scr_" + name, shape, dt).ap()
        return dram[name]

    scratch("xnT", (B, D, T), F32)
    scratch("kc", (B * TC, D), F32)
    scratch("vc", (B * TC, D), F32)
    scratch("ba", (B * TC, 2 * XH), F32)
    scratch("mem", (B, XH, XD, XD), F32)
    scratch("attT", (H * HD, TOK), F32)
    scratch("rinv", (H, B, QT, P), F32)
    scratch("x3", (TOK, D), F32)
    scratch("hs", (NE * REG, D), F32)
    scratch("ys", (NBLK * BLK, D), F32)
    scratch("tab", (4, 32), I32)
    with ExitStack() as keep:
        scan = {
            "k2": keep.enter_context(nc.sbuf_tensor("scan_k", [P, TC, XD], F32)),
            "v2": keep.enter_context(nc.sbuf_tensor("scan_v", [P, TC, XD // 2], F32)),
            "ab": keep.enter_context(nc.sbuf_tensor("scan_ab", [P, 2, TC], F32)),
        }
        context_phase(nc, io, dram, scan)
        attention_phase(nc, io, dram, scan)
    with ExitStack() as keep:
        route = {
            "pos": keep.enter_context(nc.sbuf_tensor("pos", [P, NT, 2], I32)),
            "top": keep.enter_context(nc.sbuf_tensor("top", [P, NT, 2], F32)),
            "w": keep.enter_context(nc.sbuf_tensor("w", [P, NT, 2], F32)),
            "tab": keep.enter_context(nc.sbuf_tensor("tab", [P, 4, 32], I32)),
        }
        memory_phase(nc, io, dram, route)
        expert_phase(nc, io, dram, route)
        combine_phase(nc, io, dram, route)


class Room:

    def __init__(self, nc, name):
        self.nc, self.name, self.ctx, self.sems = nc, name, ExitStack(), []

    def __enter__(self):
        return self

    def __exit__(self, *a):
        self.ctx.__exit__(*a)
        if a[0] is None:
            self.nc.clear_and_free_semaphores(self.sems)
            self.nc.all_engine_barrier()

    def sb(self, name, shape, dt=F32):
        return self.ctx.enter_context(self.nc.sbuf_tensor(self.name + name, shape, dt))

    def ps(self, name, shape, dt=F32):
        return self.ctx.enter_context(self.nc.psum_tensor(self.name + name, shape, dt))

    def sem(self, name):
        self.sems.append(self.nc.alloc_semaphore(self.name + name))
        return self.sems[-1]


def wait_alone(eng, sem, value, counter):
    eng.wait_ge(sem, value)
    eng.sem_inc(counter, 1)


class Chain:

    def __init__(self, eng, sem, base=0, counter=None):
        self.eng, self.sem, self.base, self.n, self.counter = eng, sem, base, 0, counter

    def do(self, ins):
        ins.then_inc(self.sem, 1)
        self.n += 1
        return self.n

    def sync(self):
        if self.counter is None:
            self.eng.wait_ge(self.sem, self.base + self.n)
        else:
            wait_alone(self.eng, self.sem, self.base + self.n, self.counter)

    def step(self, ins):
        self.do(ins)
        self.sync()


def context_phase(nc, io, dram, scan):
    with Room(nc, "c_") as rm:
        xt = rm.sb("xt", [P, 2, 4, D])
        xn = rm.sb("xn", [P, 2, D])
        xs = rm.sb("xs", [P, 2, ET, T // 2])
        bst = rm.sb("bst", [P, 6])
        mv = rm.sb("mv", [P, 2, 2])
        sd = rm.sb("sd", [P, 2])
        rstd = rm.sb("rstd", [P, 2])
        eps = rm.sb("eps", [P, 1])
        ctx = rm.sb("ctx", [P, CT, D])
        ctxT = rm.sb("ctxT", [P, ET, CT * P])
        wk = rm.sb("wk", [P, ET, D])
        wv = rm.sb("wv", [P, ET, D])
        wg = rm.sb("wg", [P, ET, 2 * XH])
        gb = rm.sb("gb", [P, 2 * XH])
        gk = rm.sb("gk", [P, XD])
        bk = rm.sb("bk", [P, XD])
        ident = rm.sb("ident", [P, P])
        kx = rm.sb("kx", [P, D])
        sq = rm.sb("sq", [P, D])
        kn = rm.sb("kn", [P, CT, D])
        vn = rm.sb("vn", [P, CT, D])
        st = rm.sb("st", [P, 6, XH])
        gt = rm.sb("gt", [P, CT, 2 * XH])
        gt2 = rm.sb("gt2", [P, CT, 2 * XH])
        pT = [rm.ps(f"pT{i}", [P, 512]) for i in range(2)]
        pK = rm.ps("pK", [P, 512])
        pV = rm.ps("pV", [P, 512])
        pG = rm.ps("pG", [P, 512])
        pX = [rm.ps(f"pX{i}", [P, 512]) for i in range(2)]
        s_any = rm.sem("any")
        s_eps = rm.sem("eps")
        s_x = [rm.sem(f"x{i}") for i in range(2)]
        s_bn = rm.sem("bn")
        s_mv = rm.sem("mv")
        s_sd = rm.sem("sd")
        s_rstd = rm.sem("rstd")
        s_xn = rm.sem("xn")
        s_xt = rm.sem("xt")
        s_xs = rm.sem("xs")
        s_xst = [rm.sem(f"xst{i}") for i in range(2)]
        s_xfree = rm.sem("xfree")
        s_id = rm.sem("id")
        s_in = rm.sem("in")
        s_pk = rm.sem("pk")
        s_tr = rm.sem("tr")
        s_trc = rm.sem("trc")
        s_mm = rm.sem("mm")
        s_v = rm.sem("v")
        s_sq = rm.sem("sq")
        s_dve = rm.sem("dve")
        s_kn = rm.sem("kn")
        s_g1 = rm.sem("g1")
        s_g2 = rm.sem("g2")
        s_g3 = rm.sem("g3")
        s_rt = rm.sem("rt")
        s_rs = rm.sem("rs")
        s_out = rm.sem("out")
        s_scan = rm.sem("scan")
        n_in = 16 * 7
        block = rm.ctx.enter_context(nc.Block())

        @block.sync
        def _(sp):
            sp.dma_start(ident[:, :], io["ident"]).then_inc(s_id, 16)
            sp.dma_start(ctx[:, :, :], io["ctx"].rearrange("(t p) d -> p t d", p=P)).then_inc(s_in, 16)
            for dst, src in ((wk, "wkT"), (wv, "wvT"), (wg, "wgT")):
                sp.dma_start(dst[:, :, :], io[src].rearrange("(e p) n -> p e n", p=P)).then_inc(s_in, 16)
            sp.dma_start(gb[:, :], io["gbias"].partition_broadcast(P)).then_inc(s_in, 16)
            sp.dma_start(gk[:, :], io["gk"].partition_broadcast(P)).then_inc(s_in, 16)
            sp.dma_start(bk[:, :], io["bk"].partition_broadcast(P)).then_inc(s_in, 16)
            sp.wait_ge(s_kn, CT)
            sp.wait_ge(s_v, CT)
            sp.wait_ge(s_g3, CT)
            for c in range(CT):
                rows = slice(c * P, (c + 1) * P)
                sp.dma_start(dram["kc"][rows, :], kn[:, c, :]).then_inc(s_out, 16)
                sp.dma_start(dram["vc"][rows, :], vn[:, c, :]).then_inc(s_out, 16)
                sp.dma_start(dram["ba"][rows, :], gt[:, c, :]).then_inc(s_out, 16)
            sp.wait_ge(s_out, 16 * 3 * CT)
            n = 0
            for half in range(2):
                for b in range(B):
                    p0 = half * B * XH + b * XH
                    dst = slice(p0, p0 + XH)
                    rows = slice(b * TC, (b + 1) * TC)
                    sp.dma_start(scan["k2"][dst, :, :],
                                 dram["kc"][rows, :].rearrange("t (h j) -> h t j", h=XH)).then_inc(s_scan, 16)
                    v = dram["vc"][rows, :].rearrange("t (h a i) -> h a t i", h=XH, a=2)
                    sp.dma_start(scan["v2"][dst, :, :], v[:, half]).then_inc(s_scan, 16)
                    for a in range(2):
                        sp.dma_start(scan["ab"][dst, a, :],
                                     dram["ba"][rows, a * XH:(a + 1) * XH].rearrange("t h -> h t"),
                                     allow_slow_non_contiguous=True).then_inc(s_scan, 16)
                    n += 4
            sp.wait_ge(s_scan, 16 * n)

        @block.gpsimd
        def _(gp):
            gp.memset(eps[:, :], EPS).then_inc(s_eps, 1)

            def load(b, half):
                rows = io["x"][bass.ds(b * T + half * T // 2, T // 2), :]
                gp.dma_start(xt[:, half, :, :], rows.rearrange("(j p) d -> p j d", p=P)).then_inc(s_x[half], 16)

            def batch(b, more):
                for half in range(2):
                    wait_alone(gp, s_xs, b * QT + 4 * half + 4 + CREDIT, s_any)
                    dst = dram["xnT"][bass.ds(b, 1), :, half * T // 2:(half + 1) * T // 2]
                    gp.dma_start(dst.rearrange("o (e p) t -> p (o e) t", p=P), xs[:, half, :, :]
                                 ).then_inc(s_xst[half], 16)
                    if more:
                        load(b + 1, half)
                if more:
                    for half in range(2):
                        gp.wait_ge(s_xst[half], 16 * (b + 1))
                        gp.sem_inc(s_xfree, 1)

            for half in range(2):
                load(0, half)
            with gp.Fori(0, B - 1) as b:
                batch(b, True)
            batch(B - 1, False)
            for half in range(2):
                gp.wait_ge(s_xst[half], 16 * B)

        @block.scalar
        def _(act):
            def norm_batch(b):
                def ln_scale(t):
                    act.wait_ge(s_mv, b * QT + t + 1)
                    act.activation(sd[:, t % 2:t % 2 + 1], mv[:, t % 2, 1:2], ACT.Sqrt, bias=eps[:, 0:1],
                                   scale=1.0).then_inc(s_sd, 1)

                ln_scale(0)
                for t in range(QT):
                    if t + 1 < QT:
                        ln_scale(t + 1)
                    if t % 4 == 0:
                        act.wait_ge(s_xfree, 2 * b + t // 4 - 1 + CREDIT)
                    act.wait_ge(s_xt, b * QT + t + 1)
                    act.activation(xs[:, t // 4, :, (t % 4) * P:(t % 4 + 1) * P],
                                   pX[t % 2][:, :].rearrange("p (e t) -> p e t", e=ET), ACT.Copy).then_inc(s_xs, 1)

            act.sem_inc(s_xs, CREDIT)
            act.sem_inc(s_xfree, CREDIT)
            act.wait_ge(s_eps, 1)
            norm_batch(0)
            act.wait_ge(s_in, n_in)
            for c in range(CT):
                act.wait_ge(s_tr, c + 1)
                act.activation(ctxT[:, :, c * P:(c + 1) * P], pT[c][:, :].rearrange("p (e t) -> p e t", e=ET),
                               ACT.Copy).then_inc(s_trc, 1)
            for c in range(CT):
                act.wait_ge(s_mm, 3 * c + 2)
                act.activation(vn[:, c, :], pV[:, :], ACT.Copy).then_inc(s_v, 1)
                for r in range(2):
                    act.wait_ge(s_rt, 2 * c + r + 1)
                    act.activation(st[:, 2 + 2 * r, :], st[:, 1 + 2 * r, :], ACT.Sqrt).then_inc(s_rs, 1)
            for c in range(CT):
                act.wait_ge(s_g1, c + 1)
                act.activation(gt2[:, c, :], gt[:, c, :], ACT.Exp, scale=-1.0).then_inc(s_g2, 1)
            with act.Fori(1, B) as b:
                norm_batch(b)

        @block.tensor
        def _(pe):
            def norm_batch(b):
                for t in range(QT):
                    pe.wait_ge(s_xn, b * QT + t + 1)
                    pe.wait_ge(s_xs, b * QT + t - 2 + 1 + CREDIT)
                    for e in range(ET):
                        mm = pe.transpose(pX[t % 2][:, e * P:(e + 1) * P], xn[:, t % 2, e * P:(e + 1) * P],
                                          ident[:, :])
                    mm.then_inc(s_xt, 1)

            pe.wait_ge(s_id, 16)
            norm_batch(0)
            pe.wait_ge(s_in, n_in)
            for c in range(CT):
                for e in range(ET):
                    mm = pe.transpose(pT[c][:, e * P:(e + 1) * P], ctx[:, c, e * P:(e + 1) * P], ident[:, :])
                mm.then_inc(s_tr, 1)
            for c in range(CT):
                pe.wait_ge(s_trc, c + 1)
                if c:
                    pe.wait_ge(s_pk, c)
                    pe.wait_ge(s_g1, c)
                    pe.wait_ge(s_v, c)
                for out, w, n in ((pK, wk, D), (pV, wv, D), (pG, wg, 2 * XH)):
                    for e in range(ET):
                        mm = pe.matmul(out[:, 0:n], ctxT[:, e, c * P:(c + 1) * P], w[:, e, :],
                                       start=e == 0, stop=e == ET - 1)
                    mm.then_inc(s_mm, 1)
            with pe.Fori(1, B) as b:
                norm_batch(b)

        @block.vector
        def _(dve):
            ch = Chain(dve, s_dve)
            def norm_batch(b):
                def stats(t):
                    i = b * QT + t
                    if t % 4 == 0:
                        dve.wait_ge(s_x[t // 4], 16 * (b + 1))
                    dve.bn_stats(bst[:, :], xt[:, t // 4, t % 4, :]).then_inc(s_bn, 1)
                    wait_alone(dve, s_bn, i + 1, s_any)
                    dve.bn_aggr(mv[:, t % 2, :], bst[:, :]).then_inc(s_mv, 1)
                    dve.wait_ge(s_mv, i + 1)

                def normalise(t):
                    i = b * QT + t
                    dve.wait_ge(s_sd, i + 1)
                    dve.reciprocal(rstd[:, t % 2:t % 2 + 1], sd[:, t % 2:t % 2 + 1]).then_inc(s_rstd, 1)
                    dve.wait_ge(s_rstd, i + 1)
                    if t >= 2:
                        dve.wait_ge(s_xt, i - 1)
                    dve.tensor_scalar(xn[:, t % 2, :], xt[:, t // 4, t % 4, :], mv[:, t % 2, 0:1],
                                      rstd[:, t % 2:t % 2 + 1], ALU.subtract, ALU.mult).then_inc(s_xn, 1)

                stats(0)
                for t in range(QT):
                    if t + 1 < QT:
                        stats(t + 1)
                    normalise(t)
                dve.wait_ge(s_xt, (b + 1) * QT)

            norm_batch(0)
            dve.wait_ge(s_in, n_in)

            def heads(x):
                return x.rearrange("p (h j) -> p h j", h=XH)

            def per_head(x):
                return x.unsqueeze(2).broadcast_to([P, XH, XD])

            def per_dim(x):
                return x[:, :].unsqueeze(1).broadcast_to([P, XH, XD])

            for c in range(CT):
                dve.wait_ge(s_mm, 3 * c + 1)
                ch.step(dve.tensor_reduce(st[:, 0, :], heads(pK[:, :]), AXX, ALU.add))
                ch.step(dve.tensor_scalar(st[:, 0, :], st[:, 0, :], 1.0 / XD, None, ALU.mult))
                dve.tensor_tensor(heads(kx[:, :]), heads(pK[:, :]), per_head(st[:, 0, :]),
                                  ALU.subtract).then_inc(s_pk, 1)
                dve.wait_ge(s_mm, 3 * c + 3)
                dve.tensor_tensor(gt[:, c, :], pG[:, 0:2 * XH], gb[:, :], ALU.add).then_inc(s_g1, 1)
                dve.wait_ge(s_pk, c + 1)
                ch.step(dve.tensor_tensor(sq[:, :], kx[:, :], kx[:, :], ALU.mult))
                ch.step(dve.tensor_reduce(st[:, 1, :], heads(sq[:, :]), AXX, ALU.add))
                dve.tensor_scalar(st[:, 1, :], st[:, 1, :], 1.0 / XD, EPS, ALU.mult, ALU.add).then_inc(s_rt, 1)
                dve.wait_ge(s_rs, 2 * c + 1)
                ch.step(dve.reciprocal(st[:, 5, :], st[:, 2, :]))
                ch.step(dve.tensor_tensor(heads(kx[:, :]), heads(kx[:, :]), per_head(st[:, 5, :]), ALU.mult))
                ch.step(dve.tensor_tensor(heads(kx[:, :]), heads(kx[:, :]), per_dim(gk), ALU.mult))
                ch.step(dve.tensor_tensor(heads(kx[:, :]), heads(kx[:, :]), per_dim(bk), ALU.add))
                ch.step(dve.tensor_tensor(sq[:, :], kx[:, :], kx[:, :], ALU.mult))
                dve.tensor_reduce(st[:, 3, :], heads(sq[:, :]), AXX, ALU.add).then_inc(s_rt, 1)
                dve.wait_ge(s_rs, 2 * c + 2)
                ch.step(dve.tensor_scalar(st[:, 5, :], st[:, 4, :], EPS_NORM, None, ALU.max))
                ch.step(dve.reciprocal(st[:, 5, :], st[:, 5, :]))
                dve.tensor_tensor(heads(kn[:, c, :]), heads(kx[:, :]), per_head(st[:, 5, :]),
                                  ALU.mult).then_inc(s_kn, 1)
                dve.wait_ge(s_kn, c + 1)
            for c in range(CT):
                dve.wait_ge(s_g2, c + 1)
                ch.step(dve.tensor_scalar(gt2[:, c, :], gt2[:, c, :], 1.0, None, ALU.add))
                dve.reciprocal(gt[:, c, :], gt2[:, c, :]).then_inc(s_g3, 1)
            with dve.Fori(1, B) as b:
                norm_batch(b)


def attention_phase(nc, io, dram, scan):
    with Room(nc, "a_") as rm:
        wg = rm.sb("wg", [P, 2, ET, GW], F32R)
        xT = rm.sb("xT", [P, 2, ET, T], F32R)
        cos = rm.sb("cos", [P, T])
        sin = rm.sb("sin", [P, T])
        qs = rm.sb("qs", [P, GH, T], F32R)
        kh = rm.sb("kh", [P, GH, T], F32R)
        kl = rm.sb("kl", [P, GH, T], F32R)
        v2 = rm.sb("v2", [P, QT, GH, 2, HD], F32R)
        pb = rm.sb("pb", [P, 2, T])
        pt = rm.sb("pt", [P, 2, 2, QT, 2 * P], F32R)
        otmp = rm.sb("otmp", [HD, 2, 2 * P])
        ot = rm.sb("ot", [HD, 2, 2 * P])
        raw = rm.sb("raw", [P, 2, T])
        rsum = rm.sb("rsum", [P, G * GH * QT])
        rT = rm.sb("rT", [P, P])
        nmax = rm.sb("nmax", [P, GH * QT])
        ident = rm.sb("ident", [P, P])
        identb = rm.sb("identb", [P, P], BF16)
        maskb = rm.sb("maskb", [P, P], BF16)
        ptf = pt[:, :, :, :, :].rearrange("p a b c d -> p (a b c d)")
        rot = [ptf[:, i * 4 * T:(i + 1) * 4 * T].rearrange("p (r t) -> p r t", r=4) for i in range(2)]
        tmp = pb[:, :, :].rearrange("p a (b t) -> p (a b) t", b=2)

        S = [rm.ps(f"S{i}", [P, T]) for i in range(2)]
        PT = [rm.ps(f"PT{i}", [P, 512]) for i in range(2)]
        O = [rm.ps(f"O{i}", [P, 512]) for i in range(2)]

        M = rm.sb("M", [P, XD // 2, XD])
        sp1 = rm.sb("sp1", [P, XD // 2, XD])
        bv = rm.sb("bv", [P, TC, XD // 2])
        coef = rm.sb("coef", [P, XD // 2])
        s_sc = rm.sem("sc")
        s_mem = rm.sem("mem")

        s_any = rm.sem("any")
        s_const = rm.sem("const")
        s_pool = rm.sem("pool")
        s_load = [rm.sem(f"load{i}") for i in range(2)]
        s_xload = [rm.sem(f"xload{i}") for i in range(2)]
        s_high = rm.sem("high")
        s_wlow = rm.sem("wlow")
        s_xlow = rm.sem("xlow")
        s_ptfull = rm.sem("ptfull")
        s_pthi = rm.sem("pthi")
        s_ptfree = rm.sem("ptfree")
        s_sfull = rm.sem("sfull")
        s_rel = rm.sem("rel")
        s_rop = rm.sem("rop")
        s_rhi = rm.sem("rhi")
        s_rot = rm.sem("rot")
        s_vhi = rm.sem("vhi")
        s_vlo = rm.sem("vlo")
        s_stack = [rm.sem(f"stack{i}") for i in range(GH)]
        s_gstack = [rm.sem(f"gstack{i}") for i in range(GH)]
        s_nb = rm.sem("nb")
        s_exp = rm.sem("exp")
        s_pv = rm.sem("pv")
        s_oc = rm.sem("oc")
        s_ofree = rm.sem("ofree")
        s_ost = [rm.sem(f"ost{i}") for i in range(2)]
        s_rsT = rm.sem("rsT")
        s_rinv = rm.sem("rinv")
        s_rst = rm.sem("rst")

        NP_ = GH * QT // 2
        NS = 6 + GH * QT
        uses = [(qt // 4) + 1 for qt in range(QT)]
        NPT = GH * sum(uses)

        OSLOTS = 2

        def o_slot(k):
            return O[k % 2][:, 0:2 * P]

        def pt_index(u):
            h, qt = u // QT, u % QT
            return h * sum(uses) + sum(uses[:qt])

        def weights_use(b, g):
            return 2 * ET + b * (G + 1) * ET + (g - 1) * ET

        def x_use(b):
            return ET + b * (G + 1) * ET

        def load_weights(eng, times, b, g, e):
            if e >= 2:
                wait_alone(eng, s_wlow, times * ET + e - 1, s_any)
            elif b is not None:
                wait_alone(eng, s_wlow, (times - 1) * ET + e + 3, s_any)
                wait_alone(eng, s_xlow, b * ET + e + 3, s_any)
            eng.dma_start(raw[:, e % 2, 0:GW],
                          io["wts"][bass.ds(g, 1), :, e * GW:(e + 1) * GW].rearrange("o p n -> p (o n)")
                          ).then_inc(s_load[e % 2], 16)

        def load_x(eng, times, b, e):
            if e >= 2:
                wait_alone(eng, s_xlow, times * ET + e - 1, s_any)
            else:
                wait_alone(eng, s_wlow, times * G * ET + e + 3, s_any)
            eng.dma_start(raw[:, e % 2, :],
                          dram["xnT"][bass.ds(b, 1), e * P:(e + 1) * P, :].rearrange("o p t -> p (o t)")
                          ).then_inc(s_xload[e % 2], 16)

        def high(act, sem, times, use, e, dst, cols):
            act.wait_ge(sem[e % 2], 16 * (times * ET // 2 + e // 2 + 1))
            act.activation(dst[:, 0, e, :], raw[:, e % 2, 0:cols], ACT.Copy).then_inc(s_high, 1)

        def low(eng, sem, use, e, dst, cols):
            eng.wait_ge(s_high, use + e + 1)
            eng.tensor_tensor(dst[:, 1, e, :], raw[:, e % 2, 0:cols], dst[:, 0, e, :].bitcast(F32),
                              ALU.subtract).then_inc(sem, 1)

        weight_steps = (16, 17, 24, 25)

        def wait_stack(eng, h, n):
            gps = 4 * (h < GH // 2) + 8 * (h == GH - 1)
            for sem, count in ((s_stack[h], 12 - gps), (s_gstack[h], gps)):
                if count:
                    eng.wait_ge(sem, 16 * count * (n + 1))

        def stack_k(eng, sems, h0, h1):
            for h in range(h0, h1):
                for r in range(4):
                    for dup in range(2):
                        p0 = dup * 64 + (r % 2) * 32
                        eng.dma_start((kh, kl)[r // 2][p0:p0 + 32, h, :].bitcast(F32),
                                      rot[0][h * 32:h * 32 + 32, r, :].bitcast(F32)).then_inc(sems[h], 16)

        def stack_q(eng, sems, h0, h1):
            for h in range(h0, h1):
                for r in range(4):
                    eng.dma_start(qs[r * 32:r * 32 + 32, h, :].bitcast(F32),
                                  rot[1][h * 32:h * 32 + 32, r, :].bitcast(F32)).then_inc(sems[h], 16)

        block = rm.ctx.enter_context(nc.Block())

        @block.sync
        def _(sp):
            sp.dma_start(cos[:, :], io["cos"]).then_inc(s_const, 16)
            sp.dma_start(sin[:, :], io["sin"]).then_inc(s_const, 16)
            sp.dma_start(ident[:, :], io["ident"]).then_inc(s_const, 16)
            for e in range(ET):
                load_weights(sp, 0, None, 0, e)
            with sp.Fori(0, B) as b:
                with sp.Fori(0, G) as g:
                    n = b * G + g
                    wait_alone(sp, s_rot, 4 * n + 2, s_any)
                    stack_k(sp, s_stack, 0, GH - 1)
                    wait_alone(sp, s_rot, 4 * n + 4, s_any)
                    stack_q(sp, s_stack, GH // 2, GH)
                    for e in range(2):
                        load_weights(sp, n + 1, b, (g + 1) % G, e)
                    for k in range(NP_):
                        h, pr = k // (QT // 2), k % (QT // 2)
                        wait_alone(sp, s_ofree, n * NP_ + k + 1 + OSLOTS, s_any)
                        sp.dma_start(dram["attT"][bass.ds(g * GH * HD + h * HD, HD),
                                                  bass.ds(b * T + pr * 2 * P, 2 * P)],
                                     ot[:, k % 2, :]).then_inc(s_ost[k % 2], 16)
                        if k in (6, 7):
                            load_weights(sp, n + 1, b, (g + 1) % G, k - 4)
                wait_alone(sp, s_rinv, b + 1, s_any)
                for g in range(G):
                    sp.dma_start(dram["rinv"][g * GH:(g + 1) * GH, bass.ds(b, 1), :, :]
                                 .rearrange("h o q p -> h (o q) p"),
                                 rT[g * GH * QT:(g + 1) * GH * QT, :]).then_inc(s_rst, 16)
            sp.wait_ge(s_rst, 16 * (G * B + 1))
            for i in range(2):
                sp.wait_ge(s_ost[i], 16 * (B * G * NP_ // 2 + 1))

        @block.gpsimd
        def _(gp):
            gp.memset(identb[:, :], 0.0).then_inc(s_pool, 1)
            gp.memset(maskb[:, :], 0.0).then_inc(s_pool, 1)
            gp.wait_ge(s_pool, 2)
            gp.affine_select(out=identb[:, :], in_=identb[:, :], compare_op=ALU.not_equal, fill=1.0,
                             base=0, pattern=[[-1, P]], channel_multiplier=1).then_inc(s_pool, 1)
            gp.affine_select(out=maskb[:, :], in_=maskb[:, :], compare_op=ALU.is_ge, fill=MASKED,
                             base=0, pattern=[[-1, P]], channel_multiplier=1).then_inc(s_pool, 1)
            ch = Chain(gp, s_sc)
            half = XD // 2
            ch.do(gp.memset(M[:, :, :], 0.0))
            ch.step(gp.tensor_tensor(bv[:, :, :], scan["v2"][:, :, :],
                                     scan["ab"][:, 0, :].unsqueeze(2).broadcast_to([P, TC, half]), ALU.mult))
            per = 10

            def context_row(t):
                c = Chain(gp, s_sc, t * per + ch.n, s_any)
                kt = scan["k2"][:, bass.ds(t, 1), :].broadcast_to([P, half, XD])
                c.step(gp.tensor_tensor(sp1[:, :, :], M[:, :, :], kt, ALU.mult))
                w = XD // 2
                while w:
                    c.step(gp.tensor_tensor(sp1[:, :, 0:w], sp1[:, :, 0:w], sp1[:, :, w:2 * w], ALU.add))
                    w //= 2
                c.step(gp.tensor_tensor(coef[:, :].unsqueeze(2), sp1[:, :, 0:1],
                                        scan["ab"][:, 1, bass.ds(t, 1)].unsqueeze(1).broadcast_to([P, half, 1]),
                                        ALU.mult))
                c.step(gp.tensor_tensor(coef[:, :].unsqueeze(1), bv[:, bass.ds(t, 1), :],
                                        coef[:, :].unsqueeze(1), ALU.subtract))
                c.step(gp.tensor_tensor(sp1[:, :, :], kt, coef[:, :].unsqueeze(2).broadcast_to([P, half, XD]),
                                        ALU.mult))
                c.step(gp.tensor_tensor(M[:, :, :], M[:, :, :], sp1[:, :, :], ALU.add))
                assert c.n == per

            for e in range(ET):
                low(gp, s_wlow, 0, e, wg, GW)
            for e in range(ET):
                load_x(gp, 0, 0, e)
            with gp.Fori(0, B) as b:
                with gp.Fori(0, G) as g:
                    n = b * G + g
                    wait_alone(gp, s_rot, 4 * n + 2, s_any)
                    stack_k(gp, s_gstack, GH - 1, GH)
                    wait_alone(gp, s_rot, 4 * n + 4, s_any)
                    stack_q(gp, s_gstack, 0, GH // 2)
                    with gp.Fori(0, TC // (B * G)) as i:
                        context_row(n * (TC // (B * G)) + i)
                    for e in range(ET):
                        low(gp, s_wlow, weights_use(b, g + 1), e, wg, GW)
                for e in range(ET):
                    load_x(gp, b + 1, (b + 1) % B, e)
            for a in range(2):
                gp.dma_start(dram["mem"][:, :, a * half:(a + 1) * half, :].rearrange("b h i j -> (b h) (i j)"),
                             M[a * 64:(a + 1) * 64, :, :].rearrange("p i j -> p (i j)")).then_inc(s_mem, 16)
            gp.wait_ge(s_mem, 32)

        @block.tensor
        def _(pe):
            pe.sem_inc(s_pv, CREDIT)
            pe.wait_ge(s_const, 48)
            pe.wait_ge(s_pool, 4)

            def split_mm(out, lhs, rhs, start, stop):
                pe.matmul(out, lhs(0), rhs(0), start=start, stop=False)
                pe.matmul(out, lhs(0), rhs(1), start=False, stop=False)
                return pe.matmul(out, lhs(1), rhs(0), start=False, stop=stop)

            with pe.Fori(0, B) as b:
                with pe.Fori(0, G) as g:
                    n = b * G + g
                    pt0 = n * NPT
                    pe.wait_ge(s_wlow, ET * (n + 1))
                    pe.wait_ge(s_xlow, ET * (b + 1))
                    for j in range(4):
                        col0, c = (1 - j // 2) * 2 * P, j % 2
                        if j < 2:
                            pe.wait_ge(s_exp, 32 * n + j - 1 + CREDIT)
                        else:
                            pe.wait_ge(s_rel, 6 * n + j - 1)
                        for a in range(2):
                            for e in range(ET):
                                mm = split_mm(S[j % 2][:, a * 512:(a + 1) * 512],
                                              lambda i: wg[:, i, e, col0 + a * P:col0 + (a + 1) * P],
                                              lambda i: xT[:, i, e, c * 512:(c + 1) * 512],
                                              e == 0, e == ET - 1)
                        mm.then_inc(s_sfull, 1)
                    for j in range(4, 6):
                        pe.wait_ge(s_rel, 6 * n + j - 1)
                        for tt in range(4):
                            t = (j - 4) * 4 + tt
                            for e in range(ET):
                                mm = split_mm(S[j % 2][:, tt * 256:(tt + 1) * 256],
                                              lambda i: xT[:, i, e, t * P:(t + 1) * P],
                                              lambda i: wg[:, i, e, 4 * P:6 * P],
                                              e == 0, e == ET - 1)
                        mm.then_inc(s_sfull, 1)

                    def scores(u):
                        h, qt = u // QT, u % QT
                        if qt == 0:
                            wait_stack(pe, h, n)
                        if u < 2:
                            pe.wait_ge(s_rel, 6 * n + 4 + u + 1)
                        else:
                            pe.wait_ge(s_exp, 32 * n + u - 1 + CREDIT)
                        q = qs[:, h, qt * P:(qt + 1) * P]
                        cols = (qt + 1) * P
                        for c0 in range(0, cols, 512):
                            c1 = min(cols, c0 + 512)
                            out = S[u % 2][:, c0:c1]
                            last = c1 == cols
                            pe.matmul(out, q, kh[:, h, c0:c1], start=True, stop=False)
                            mm = pe.matmul(out, q, kl[:, h, c0:c1], start=False, stop=not last)
                        mm = pe.matmul(S[u % 2][:, cols - P:cols], identb[:, :], maskb[:, :],
                                       start=False, stop=True)
                        mm.then_inc(s_sfull, 1)

                    def turn(u):
                        h, qt = u // QT, u % QT
                        pe.wait_ge(s_exp, 32 * n + u + 1 + CREDIT)
                        k = pt_index(u)
                        for s in range(uses[qt]):
                            pe.wait_ge(s_ptfree, pt0 + k + s + 1)
                            for kt in range(4 * s, min(qt + 1, 4 * s + 4)):
                                mm = pe.transpose(PT[(k + s) % 2][:, (kt % 4) * P:(kt % 4 + 1) * P],
                                                  pb[:, u % 2, kt * P:(kt + 1) * P], ident[:, :])
                            mm.then_inc(s_ptfull, 1)

                    def values(k, part):
                        h, pr = k // (QT // 2), k % (QT // 2)
                        last = pt_index(2 * k + 1) + uses[(2 * k + 1) % QT]
                        if part == 0:
                            pe.wait_ge(s_pthi, pt0 + last)
                            pe.wait_ge(s_ofree, n * NP_ + k + 1)
                            if k == 0:
                                pe.wait_ge(s_vlo, 2 * (n + 1))
                        else:
                            pe.wait_ge(s_ptfree, pt0 + last + CREDIT)
                        nk = 2 * pr + 2
                        for kt in range(nk):
                            c0 = P if kt == nk - 1 else 0
                            mm = pe.matmul(o_slot(k)[:, c0:2 * P],
                                           v2[:, kt, h, :, :].rearrange("p a d -> p (a d)"),
                                           pt[:, k % 2, part, kt, c0:2 * P],
                                           start=kt == 0 and part == 0, stop=kt == nk - 1 and part == 1)
                        if part == 1:
                            mm.then_inc(s_pv, 1)

                    for u in range(GH * QT + 4):
                        if u < GH * QT:
                            scores(u)
                        if 2 <= u < GH * QT + 2:
                            turn(u - 2)
                        if u >= 4:
                            values((u - 4) // 2, u % 2)
                pe.wait_ge(s_ofree, (b + 1) * G * NP_ + OSLOTS)
                pe.wait_ge(s_exp, (b + 1) * G * 32 + CREDIT)
                pe.transpose(O[0][:, 0:P], rsum[:, :], ident[:, :]).then_inc(s_rsT, 1)
                pe.wait_ge(s_rinv, b + 1)

        @block.scalar
        def _(act):
            act.sem_inc(s_exp, CREDIT)

            for e in range(ET):
                high(act, s_load, 0, 0, e, wg, GW)
            for e in range(ET):
                high(act, s_xload, 0, ET, e, xT, T)
            with act.Fori(0, B) as b:
                with act.Fori(0, G) as g:
                    n = b * G + g
                    pt0 = n * NPT
                    for j in range(4):
                        for r in range(2):
                            act.wait_ge(s_rop, n * 24 + j * 6 + 3 * r + 3)
                            act.activation(rot[j // 2][:, r, (j % 2) * 512:(j % 2 + 1) * 512],
                                           tmp[:, 2 * r, :], ACT.Copy, scale=SCALE if j >= 2 else 1.0
                                           ).then_inc(s_rhi, 1)
                    for j in range(2):
                        act.wait_ge(s_sfull, n * NS + 5 + j)
                        act.activation(v2[:, 4 * j:4 * j + 4, :, 0, :],
                                       S[j % 2][:, :].rearrange("p (t h d) -> p t h d", t=4, h=GH),
                                       ACT.Copy).then_inc(s_vhi, 1)

                    def exps(u):
                        h, qt = u // QT, u % QT
                        act.wait_ge(s_nb, 32 * n + u + 1)
                        if u < 2:
                            act.wait_ge(s_rot, 4 * (n + 1))
                        else:
                            act.wait_ge(s_ptfull, pt0 + pt_index(u - 2) + uses[(u - 2) % QT])
                        cols = (qt + 1) * P
                        act.activation(pb[:, u % 2, 0:cols], S[u % 2][:, 0:cols], ACT.Exp,
                                       bias=nmax[:, u:u + 1], scale=1.0,
                                       accum_out=rsum[:, bass.ds(g * GH * QT + u, 1)]).then_inc(s_exp, 1)

                    def part_high(u):
                        h, qt = u // QT, u % QT
                        k = pt_index(u)
                        if u == 0:
                            for i in range(GH):
                                wait_stack(act, i, n)
                        if u % 2 == 0:
                            act.wait_ge(s_pv, NP_ * n + u // 2 - 1 + CREDIT)
                        for s in range(uses[qt]):
                            m = min(4, qt + 1 - 4 * s)
                            act.wait_ge(s_ptfull, pt0 + k + s + 1)
                            act.activation(pt[:, (u // 2) % 2, 0, 4 * s:4 * s + m, (u % 2) * P:(u % 2 + 1) * P],
                                           PT[(k + s) % 2][:, 0:m * P].rearrange("p (k q) -> p k q", k=m),
                                           ACT.Copy).then_inc(s_pthi, 1)

                    def out_low(k):
                        act.wait_ge(s_pv, NP_ * n + k + 1 + CREDIT)
                        act.wait_ge(s_ofree, n * NP_ + k - 1 + OSLOTS)
                        act.activation(otmp[:, k % 2, :], o_slot(k)[HD:P, :], ACT.Copy).then_inc(s_oc, 1)

                    for u in range(GH * QT + 6):
                        if 2 <= u < GH * QT + 2:
                            part_high(u - 2)
                        if u < GH * QT:
                            exps(u)
                        if u >= 6 and u % 2 == 0:
                            out_low((u - 6) // 2)
                        if u in weight_steps:
                            if u == weight_steps[0]:
                                act.wait_ge(s_sfull, n * NS + 6)
                            high(act, s_load, n + 1, weights_use(b, g + 1), weight_steps.index(u), wg, GW)
                act.wait_ge(s_sfull, (b * G + G - 1) * NS + 6)
                for e in range(ET):
                    high(act, s_xload, b + 1, x_use(b + 1), e, xT, T)

        @block.vector
        def _(dve):
            dve.sem_inc(s_ptfree, CREDIT)
            dve.sem_inc(s_ofree, OSLOTS)
            dve.sem_inc(s_ost[0], 16)
            dve.sem_inc(s_ost[1], 16)
            dve.sem_inc(s_rst, 16)
            dve.wait_ge(s_const, 48)

            for e in range(ET):
                low(dve, s_xlow, ET, e, xT, T)
            with dve.Fori(0, B) as b:
                with dve.Fori(0, G) as g:
                    n = b * G + g
                    pt0 = n * NPT
                    for j in range(4):
                        c = j % 2
                        cs, sn = cos[:, c * 512:(c + 1) * 512], sin[:, c * 512:(c + 1) * 512]
                        x1, x2 = S[j % 2][:, 0:512], S[j % 2][:, 512:1024]
                        dve.wait_ge(s_sfull, n * NS + j + 1)
                        r0 = n * 24 + j * 6
                        dve.tensor_tensor(tmp[:, 0, :], x1, cs, ALU.mult).then_inc(s_rop, 1)
                        dve.tensor_tensor(tmp[:, 1, :], x2, sn, ALU.mult).then_inc(s_rop, 1)
                        dve.wait_ge(s_rop, r0 + 2)
                        dve.tensor_tensor(tmp[:, 0, :], tmp[:, 0, :], tmp[:, 1, :], ALU.subtract).then_inc(s_rop, 1)
                        dve.tensor_tensor(tmp[:, 2, :], x1, sn, ALU.mult).then_inc(s_rop, 1)
                        dve.tensor_tensor(tmp[:, 3, :], x2, cs, ALU.mult).then_inc(s_rop, 1)
                        dve.wait_ge(s_rop, r0 + 5)
                        dve.sem_inc(s_rel, 1)
                        dve.tensor_tensor(tmp[:, 2, :], tmp[:, 2, :], tmp[:, 3, :], ALU.add).then_inc(s_rop, 1)
                        for r in range(2):
                            dve.wait_ge(s_rhi, n * 8 + j * 2 + r + 1)
                            o = slice(c * 512, (c + 1) * 512)
                            hi = rot[j // 2][:, r, o].bitcast(F32)
                            if j >= 2:
                                ins = dve.scalar_tensor_tensor(out=rot[1][:, 2 + r, o], in0=tmp[:, 2 * r, :],
                                                               scalar=SCALE, in1=hi, op0=ALU.mult,
                                                               op1=ALU.subtract)
                            else:
                                ins = dve.tensor_tensor(rot[0][:, 2 + r, o], tmp[:, 2 * r, :], hi, ALU.subtract)
                        ins.then_inc(s_rot, 1)
                        dve.wait_ge(s_rot, 4 * n + j + 1)
                    for j in range(2):
                        dve.wait_ge(s_vhi, 2 * n + j + 1)
                        src = S[j % 2][:, :].rearrange("p (t h d) -> p t h d", t=4, h=GH)
                        dve.tensor_tensor(v2[:, 4 * j:4 * j + 4, :, 1, :], src,
                                          v2[:, 4 * j:4 * j + 4, :, 0, :].bitcast(F32),
                                          ALU.subtract).then_inc(s_vlo, 1)
                        dve.wait_ge(s_vlo, 2 * n + j + 1)
                        dve.sem_inc(s_rel, 1)

                    def rowmax(u):
                        cols = (u % QT + 1) * P
                        dve.wait_ge(s_sfull, n * NS + 6 + u + 1)
                        dve.tensor_reduce(nmax[:, u:u + 1], S[u % 2][:, 0:cols], AXX, ALU.max,
                                          negate=True).then_inc(s_nb, 1)

                    def part_low(u):
                        h, qt = u // QT, u % QT
                        k = pt_index(u)
                        for s in range(uses[qt]):
                            m = min(4, qt + 1 - 4 * s)
                            dve.wait_ge(s_pthi, pt0 + k + s + 1)
                            q = slice((u % 2) * P, (u % 2 + 1) * P)
                            dve.tensor_tensor(pt[:, (u // 2) % 2, 1, 4 * s:4 * s + m, q],
                                              PT[(k + s) % 2][:, 0:m * P].rearrange("p (k q) -> p k q", k=m),
                                              pt[:, (u // 2) % 2, 0, 4 * s:4 * s + m, q].bitcast(F32),
                                              ALU.subtract).then_inc(s_ptfree, 1)

                    def out_sum(k):
                        dve.wait_ge(s_oc, n * NP_ + k + 1)
                        dve.wait_ge(s_ost[k % 2], 16 * (NP_ // 2 * n + k // 2) + 16)
                        dve.tensor_tensor(ot[:, k % 2, :], o_slot(k)[0:HD, :], otmp[:, k % 2, :],
                                          ALU.add).then_inc(s_ofree, 1)

                    for u in range(GH * QT + 6):
                        if u < GH * QT:
                            rowmax(u)
                        if u >= 7 and u % 2 == 1:
                            out_sum((u - 7) // 2)
                        if 2 <= u < GH * QT + 2:
                            part_low(u - 2)
                for e in range(ET):
                    low(dve, s_xlow, x_use(b + 1), e, xT, T)
                dve.wait_ge(s_rsT, b + 1)
                dve.wait_ge(s_rst, 16 * G * b + 16)
                dve.reciprocal(rT[:, :], O[0][:, 0:P]).then_inc(s_rinv, 1)


def memory_phase(nc, io, dram, route):
    with Room(nc, "m_") as rm:
        ww = rm.sb("ww", [P, 2, 2 * WCOLS], F32R)
        mw = rm.sb("mw", [P, 2, ET, D], F32R)
        bd = rm.sb("bd", [P, XH // 4, P])
        wo = rm.sb("wo", [P, ET, D])
        att = rm.sb("att", [P, 2, 8, P])
        rb = rm.sb("rb", [P, 2, 8, P])
        ap = rm.sb("ap", [P, 2, 2, 8, P], F32R)
        x = rm.sb("x", [P, 2, D])
        x2 = rm.sb("x2", [P, 2, D])
        x2b = rm.sb("x2b", [P, 4, D])
        n2 = rm.sb("n2", [P, 2, D])
        nT = rm.sb("nT", [P, 2, 2, ET, P], F32R)
        qc = rm.sb("qc", [P, 2, D])
        sq = rm.sb("sq", [P, D])
        qn = rm.sb("qn", [P, 2, D])
        qf = rm.sb("qf", [P, D])
        qT = rm.sb("qT", [P, 2, 2, ET, P], F32R)
        x3 = rm.sb("x3", [P, 2, D])
        hn = rm.sb("hn", [P, QT, D])
        hT = rm.sb("hT", [P, 2, ET, P])
        rw = rm.sb("rw", [P, ET, NE])
        rbias = rm.sb("rbias", [P, NE])
        bo = rm.sb("bo", [P, D])
        gq = rm.sb("gq", [P, 1])
        bq = rm.sb("bq", [P, 1])
        ident = rm.sb("ident", [P, P])
        zero = rm.sb("zero", [P, D])
        eps = rm.sb("eps", [P, 1])
        tri = rm.sb("tri", [P, P], BF16)
        ones = rm.sb("ones", [P, P], BF16)
        iota8 = rm.sb("iota8", [P, NE])
        base = rm.sb("base", [P, NE])
        it = rm.sb("it", [P, 32], I32)
        itf = rm.sb("itf", [P, 32])
        st = rm.sb("st", [P, 2, 6])
        mv = rm.sb("mv", [P, 2, 2])
        sd = rm.sb("sd", [P, 2])
        rs = rm.sb("rs", [P, 2])
        hs1 = rm.sb("hs1", [P, 2, XH])
        hs2 = rm.sb("hs2", [P, 2, XH])
        hs3 = rm.sb("hs3", [P, 2, XH])
        lg = rm.sb("lg", [P, NE])
        top8 = rm.sb("top8", [P, QT, NE])
        ix8 = rm.sb("ix8", [P, NE], U32)
        idx = rm.sb("idx", [P, 2, NE])
        m1 = rm.sb("m1", [P, NE])
        msum = rm.sb("msum", [P, 2, NE], BF16)
        cum = rm.sb("cum", [P, NE], BF16)
        pr = rm.sb("pr", [P, NE])
        junk = rm.sb("junk", [P, NE])
        pf = rm.sb("pf", [P, 2, 2])
        pi = rm.sb("pi", [P, QT, 2], I32)
        cnt = rm.sb("cnt", [P, NE])
        nb = rm.sb("nb", [P, NE])
        end = rm.sb("end", [P, NE])
        tb = rm.sb("tb", [P, 8, 32])
        e2 = rm.sb("e2", [P, NT])
        tp = rm.sb("tp", [P, 3, 2 * NT])
        pA = [rm.ps(f"A{i}", [P, 512]) for i in range(2)]
        pQ, pM, pR, pW = (rm.ps(n, [P, 512]) for n in "QMRW")
        pT = [rm.ps(f"T{i}", [P, 512]) for i in range(2)]

        names = (
            "any c pool w wh wl "
            "bd mwp mwh mwl "
            "attl0 attl1 xl0 xl1 "
            "an ahi alo A x2 x2b "
            "bn mv sd rs n2 hn "
            "T nhi nlo Q "
            "hmean qc sq hvar hsd hrs qn "
            "qf qhi qlo M x3 "
            "hT R rt dc ms rank cumd cnt pos "
            "sc0 sc1 sc2 sc3 scd "
            "st30 st31 keep "
            "e tot tb fin zero"
        ).split()
        s = {k: rm.sem(k) for k in names}
        WPIECE = 2 * WCOLS // 3
        hnf = hn[:, :, :].rearrange("p t d -> p (t d)")
        wraw = [hnf[:, 0:WPIECE], hnf[:, WPIECE:2 * WPIECE], x2b[:, :, :].rearrange("p t d -> p (t d)")]
        CR = 2
        LAG = 4

        def sweep(eng, step):
            for i in range(LAG):
                step(0, i)
            with eng.Fori(0, B - 1) as r:
                for i in range(LAG, LAG + QT):
                    step(r, i)
            for i in range(LAG, LAG + QT):
                step(B - 1, i)

        def here(r, j):
            return j >= 0 and (not isinstance(r, int) or r * QT + j < NT)

        def after(r, j, n):
            return not isinstance(r, int) or r * QT + j >= n

        def nth(seq, r, per_step, a, b):
            if isinstance(r, int):
                return seq.index((a, r * QT + b)), 0
            return seq.index((a, b)), r * QT * per_step

        turns = [(k, i - d) for i in range(NT + LAG) for k, d in (("n", 1), ("q", 2), ("h", 3)) if 0 <= i - d < NT]
        done = {"n": "nlo", "q": "qf", "h": "hT"}

        def wait_turn(eng, r, kind, j):
            at, _ = nth(turns, r, 3, kind, j)
            if at >= 2:
                k, t = turns[at - 2]
                eng.wait_ge(s[done[k]], (0 if isinstance(r, int) else r * QT) + t + 1 + CR)

        def slot(kind, r, j):
            return nth(turns, r, 3, kind, j)[0] % 2

        def turned(kind, r, j):
            at, base = nth(turns, r, 3, kind, j)
            return base + at + 1 + CR

        order = [(k, i) for i in range(NT + LAG) for k in range(2) if 0 <= i - 2 * k < NT]

        def lnorm(r, i, k):
            at, base = nth(order, r, 2, k, i)
            return base + at + 1

        def memory_of(r, i):
            if i == 2:
                return 0
            return r + 1 if i == 2 + QT and here(r, QT) else None

        def product_bank(i, q):
            return (pA[(i + 1) % 2], pM)[q % 2]

        block = rm.ctx.enter_context(nc.Block())

        @block.sync
        def _(sp):
            for i in range(3):
                for a in range(2):
                    c0, c1 = max(i * WPIECE, a * WCOLS), min((i + 1) * WPIECE, (a + 1) * WCOLS)
                    if c0 < c1:
                        sp.dma_start(wraw[i][:, c0 - i * WPIECE:c1 - i * WPIECE],
                                     io["wts"][G + a][:, c0 - a * WCOLS:c1 - a * WCOLS]).then_inc(s["w"], 16)
            for dst, src in ((wo[:, :, :], io["woT"].rearrange("(e p) n -> p e n", p=P)),
                             (rw[:, :, :], io["rw"].rearrange("(e p) n -> p e n", p=P)),
                             (rbias[:, :], io["rb"].partition_broadcast(P)),
                             (bo[:, :], io["bo"].partition_broadcast(P)),
                             (gq[:, :], io["gq"]), (bq[:, :], io["bq"]), (ident[:, :], io["ident"])):
                sp.dma_start(dst, src).then_inc(s["c"], 16)
            sp.wait_ge(s["pool"], 6)

            def load_memory(b):
                for h in range(4):
                    src = dram["mem"][bass.ds(b, 1)].rearrange("o (q h) i j -> h (o i) q j", h=4)[h]
                    sp.dma_start(bd[32 * h:32 * h + 32, :, 32 * h:32 * h + 32], src).then_inc(s["bd"], 16)

            def load(r, j):
                t = r * QT + j
                wait_alone(sp, s["ahi"], t - 1 + CR, s["any"])
                wait_alone(sp, s["alo"], t - 1 + CR, s["any"])
                wait_alone(sp, s["x2"], t - 1 + CR, s["any"])
                a = dram["attT"][:, bass.ds(t * P, P)].rearrange("(f p) t -> p f t", p=P)
                sp.dma_start(att[:, j % 2, :, :], a).then_inc(s[f"attl{j % 2}"], 16)
                d = dram["rinv"].rearrange("h b q p -> h (b q) p")[:, bass.ds(t, 1), :]
                d = d.rearrange("(f a) o p -> a (o f) p", a=2)
                for a in range(2):
                    sp.dma_start(rb[a * 64:(a + 1) * 64, j % 2, :, :],
                                 d[a].partition_broadcast(64)).then_inc(s[f"attl{j % 2}"], 16)
                sp.dma_start(x[:, j % 2, :], io["x"][bass.ds(t * P, P), :]).then_inc(s[f"xl{j % 2}"], 16)

            def step(r, i):
                if i == LAG and here(r, QT):
                    wait_alone(sp, s["mwp"], 4 * (r + 1) + CR, s["any"])
                    load_memory(r + 1)
                if here(r, i + 2):
                    load(r, i + 2)
                if here(r, i - 2):
                    t = r * QT + i - 2
                    wait_alone(sp, s["x3"], t + 1 + CR, s["any"])
                    sp.dma_start(dram["x3"][bass.ds(t * P, P), :], x3[:, i % 2, :]).then_inc(s[f"st3{i % 2}"], 16)

            load_memory(0)
            for j in range(2):
                load(0, j)
            sweep(sp, step)
            for i in range(2):
                sp.wait_ge(s[f"st3{i}"], 16 * (B * QT // 2 + 1))
            sp.wait_ge(s["fin"], 1)
            for e in range(NE):
                z = sp.value_load(route["tab"][0:1, 3, e:e + 1], min_val=0, max_val=(NE - 1) * REG + TOK)
                sp.dma_start(dram["hs"][bass.ds(z, BLK), :].rearrange("(a p) d -> p a d", p=P),
                             zero[:, :].unsqueeze(1).broadcast_to([P, BLK // P, D])).then_inc(s["zero"], 16)
            sp.wait_ge(s["zero"], 16 * NE)

        @block.gpsimd
        def _(gp):
            pool = Chain(gp, s["pool"])
            pool.do(gp.memset(bd[:, :, :], 0.0))
            pool.do(gp.memset(zero[:, :], 0.0))
            pool.do(gp.memset(eps[:, :], EPS))
            pool.do(gp.memset(tri[:, :], 1.0))
            pool.do(gp.memset(ones[:, :], 1.0))
            pool.do(gp.memset(cum[:, :], 0.0))
            pool.do(gp.iota(it[:, :], pattern=[[1, 32]], base=0, channel_multiplier=0))
            pool.sync()
            pool.do(gp.affine_select(out=tri[:, :], in_=tri[:, :], compare_op=ALU.is_ge, fill=0.0,
                                     base=-1, pattern=[[1, P]], channel_multiplier=-1))
            pool.step(gp.tensor_copy(itf[:, :], it[:, :]))
            pool.do(gp.tensor_copy(iota8[:, :], itf[:, 0:NE]))
            pool.step(gp.tensor_scalar(base[:, :], itf[:, 0:NE], float(REG), None, ALU.mult))
            gp.wait_ge(s["c"], 16 * 7)
            gp.sem_inc(s["scd"], QT)

            def att_scale(r, j):
                gp.wait_ge(s[f"attl{j % 2}"], 48 * (r * QT // 2 + j // 2 + 1))
                gp.tensor_tensor(att[:, j % 2, :, :], att[:, j % 2, :, :], rb[:, j % 2, :, :],
                                 ALU.mult).then_inc(s["an"], 1)

            def step(r, i):
                t = r * QT + i
                if here(r, i):
                    gp.wait_ge(s["x2"], t + 1 + CR)
                    if after(r, i, 4):
                        gp.wait_ge(s["x3"], t - 3 + CR)
                    gp.tensor_tensor(x2b[:, i % 4, :], x2[:, i % 2, :], bo[:, :], ALU.add).then_inc(s["x2b"], 1)
                if here(r, i - 1):
                    j = i - 1
                    gp.wait_ge(s["hrs"], t)
                    if after(r, j, 2):
                        gp.wait_ge(s["T"], turned("q", r, j - 2))
                    gp.tensor_tensor(qn[:, j % 2, :].rearrange("p (h j) -> p h j", h=XH),
                                     qc[:, j % 2, :].rearrange("p (h j) -> p h j", h=XH),
                                     hs3[:, j % 2, :].unsqueeze(2).broadcast_to([P, XH, XD]),
                                     ALU.mult).then_inc(s["qn"], 1)
                if here(r, i + 2):
                    att_scale(r, i + 2)
                if here(r, i - 4):
                    j = i - 4
                    wait_alone(gp, s["pos"], t - 4 + 1 + CR, s["any"])
                    for k in range(2):
                        gp.indirect_dma_start(dram["hs"][:, :],
                                              bass.IndirectOffsetOnAxis(ap=pi[:, j % QT, k:k + 1], axis=0),
                                              hn[:, j % QT, :], None).then_inc(s[f"sc{j % 4}"], 16)
                    if after(r, j, 2):
                        gp.wait_ge(s[f"sc{(j - 2) % 4}"], 32 * (r * QT // 4 + (j - 2) // 4 + 1))
                        gp.sem_inc(s["scd"], 1)

            for j in range(2):
                att_scale(0, j)
            sweep(gp, step)
            for k in range(4):
                gp.wait_ge(s[f"sc{k}"], 32 * NT // 4)

        @block.tensor
        def _(pe):
            pe.sem_inc(s["mwp"], CR)
            pe.sem_inc(s["T"], CR)
            pe.wait_ge(s["wl"], 3)
            pe.wait_ge(s["c"], 16 * 7)
            pe.wait_ge(s["pool"], 11)

            def parts(out, lhs, rhs, k, n):
                pe.matmul(out, lhs(0), rhs(0), start=k == 0, stop=False)
                pe.matmul(out, lhs(0), rhs(1), start=False, stop=False)
                return pe.matmul(out, lhs(1), rhs(0), start=False, stop=k == n - 1)

            def step(r, i):
                t = r * QT + i

                def turn(kind, lag, src, ready):
                    pe.wait_ge(s[ready], t - lag + 1)
                    wait_turn(pe, r, kind, i - lag)
                    for e in range(ET):
                        mm = pe.transpose(pT[slot(kind, r, i - lag)][:, e * P:(e + 1) * P],
                                          src[:, e * P:(e + 1) * P], ident[:, :])
                    mm.then_inc(s["T"], 1)

                def att_out(f0, f1):
                    for f in range(f0, f1):
                        mm = parts(pA[i % 2][:, :], lambda a: ap[:, i % 2, a, f, :],
                                   lambda a: ww[:, a, f * D:(f + 1) * D], f, 8)
                    return mm

                if here(r, i - 1):
                    turn("n", 1, n2[:, (i - 1) % 2, :], "n2")
                if here(r, i):
                    pe.wait_ge(s["alo"], t + 1 + CR)
                    pe.wait_ge(s["x2"], t - 1 + CR)
                    att_out(0, 4)
                if here(r, i - 2):
                    turn("q", 2, qn[:, (i - 2) % 2, :], "qn")
                if here(r, i):
                    att_out(4, 8).then_inc(s["A"], 1)
                b = memory_of(r, i)
                if b is not None:
                    pe.wait_ge(s["bd"], 64 * (b + 1))
                    pe.wait_ge(s["x2"], t + CR)
                    if here(r, i - 3):
                        pe.wait_ge(s["x3"], t - 2 + CR)
                    for q in range(4):
                        if q >= 2:
                            pe.wait_ge(s["mwl"], 4 * b + q - 1 + CR)
                        pe.matmul(product_bank(i, q)[:, :], bd[:, q, :], wo[:, q, :], start=True, stop=True
                                  ).then_inc(s["mwp"], 1)
                if here(r, i - 3):
                    turn("h", 3, hn[:, (i - 3) % QT, :], "hn")
                if here(r, i - 4):
                    pe.wait_ge(s["ms"], t - 4 + 1)
                    pe.wait_ge(s["pos"], t - 4 + CR)
                    pe.matmul(pW[:, 0:NE], tri[:, :], msum[:, i % 2, :], start=True, stop=False)
                    pe.matmul(pW[:, 0:NE], ones[:, :], cum[:, :], start=False, stop=True
                              ).then_inc(s["rank"], 1)
                if here(r, i - 1):
                    pe.wait_ge(s["nlo"], t + CR)
                    pe.wait_ge(s["qc"], t - 1 + CR)
                    for e in range(ET):
                        mm = parts(pQ[:, :], lambda a: nT[:, (i - 1) % 2, a, e, :],
                                   lambda a: ww[:, a, (8 + e) * D:(9 + e) * D], e, ET)
                    mm.then_inc(s["Q"], 1)
                if here(r, i - 2):
                    pe.wait_ge(s["qlo"], t - 1)
                    pe.wait_ge(s["x3"], t - 2 + CR)
                    if b is not None:
                        pe.wait_ge(s["mwl"], 4 * (b + 1) + CR)
                    for e in range(ET):
                        mm = parts(pM[:, :], lambda a: qT[:, i % 2, a, e, :],
                                   lambda a: mw[:, a, e, :], e, ET)
                    mm.then_inc(s["M"], 1)
                if here(r, i - 3):
                    pe.wait_ge(s["hT"], t - 2 + CR)
                    pe.wait_ge(s["rt"], t - 3 + CR)
                    for e in range(ET):
                        mm = pe.matmul(pR[:, 0:NE], hT[:, (i - 3) % 2, e, :], rw[:, e, :],
                                       start=e == 0, stop=e == ET - 1)
                    mm.then_inc(s["R"], 1)

            sweep(pe, step)
            pe.wait_ge(s["pos"], NT + CR)
            pe.matmul(pW[:, 0:NE], ones[:, :], cum[:, :], start=True, stop=True).then_inc(s["tot"], 1)

        @block.scalar
        def _(act):
            act.sem_inc(s["qf"], CR)
            act.sem_inc(s["hT"], CR)
            act.sem_inc(s["ahi"], CR)
            act.wait_ge(s["w"], 64)
            for i in range(3):
                act.activation(ww[:, 0, i * WPIECE:(i + 1) * WPIECE], wraw[i], ACT.Copy).then_inc(s["wh"], 1)
            act.wait_ge(s["c"], 16 * 7)
            act.wait_ge(s["pool"], 11)
            def att_high(r, j):
                t = r * QT + j
                act.wait_ge(s["an"], t + 1)
                act.wait_ge(s["x2"], t - 1 + CR)
                act.activation(ap[:, j % 2, 0, :, :], att[:, j % 2, :, :], ACT.Copy).then_inc(s["ahi"], 1)

            def step(r, i):
                t = r * QT + i
                if here(r, i - 1):
                    act.wait_ge(s["T"], turned("n", r, i - 1))
                    act.wait_ge(s["qc"], t - 2 + CR)
                    act.activation(nT[:, (i - 1) % 2, 0, :, :],
                                   pT[slot("n", r, i - 1)][:, :].rearrange("p (e t) -> p e t", e=ET),
                                   ACT.Copy).then_inc(s["nhi"], 1)
                if here(r, i - 2):
                    act.wait_ge(s["T"], turned("q", r, i - 2))
                    if after(r, i - 2, 1):
                        act.wait_ge(s["qlo"], t - 2)
                    act.activation(qf[:, :], pT[slot("q", r, i - 2)][:, :], ACT.Identity, bias=bq[:, 0:1],
                                   scale=gq[:, 0:1]).then_inc(s["qf"], 1)
                    act.wait_ge(s["x3"], t - 3 + CR)
                    act.wait_ge(s["qf"], t - 1 + CR)
                    act.activation(qT[:, i % 2, 0, :, :], qf[:, :].rearrange("p (e t) -> p e t", e=ET),
                                   ACT.Copy).then_inc(s["qhi"], 1)
                if here(r, i + 1):
                    att_high(r, i + 1)
                if here(r, i):
                    act.wait_ge(s["mv"], lnorm(r, i, 0))
                    act.activation(sd[:, 0:1], mv[:, 0, 1:2], ACT.Sqrt, bias=eps[:, 0:1]).then_inc(s["sd"], 1)
                b = memory_of(r, i)
                if b is not None:
                    for q in range(4):
                        act.wait_ge(s["mwp"], 4 * b + q + 1 + CR)
                        act.activation(mw[:, 0, q, :], product_bank(i, q)[:, :], ACT.Copy).then_inc(s["mwh"], 1)
                if here(r, i - 3):
                    act.wait_ge(s["T"], turned("h", r, i - 3))
                    act.wait_ge(s["rt"], t - 4 + CR)
                    act.activation(hT[:, (i - 3) % 2, :, :],
                                   pT[slot("h", r, i - 3)][:, :].rearrange("p (e t) -> p e t", e=ET),
                                   ACT.Copy).then_inc(s["hT"], 1)
                if here(r, i - 1):
                    act.wait_ge(s["qc"], t + CR)
                    act.activation(sq[:, :], qc[:, (i - 1) % 2, :], ACT.Square).then_inc(s["sq"], 1)
                    act.wait_ge(s["hvar"], 2 * t)
                    act.activation(hs2[:, (i - 1) % 2, :], hs1[:, (i - 1) % 2, :], ACT.Sqrt, bias=eps[:, 0:1],
                                   scale=1.0 / XD).then_inc(s["hsd"], 1)
                if here(r, i - 2):
                    act.wait_ge(s["mv"], lnorm(r, i, 1))
                    act.activation(sd[:, 1:2], mv[:, 1, 1:2], ACT.Sqrt, bias=eps[:, 0:1]).then_inc(s["sd"], 1)

            att_high(0, 0)
            sweep(act, step)
            act.wait_ge(s["e"], 1)
            act.activation(e2[:, :], e2[:, :], ACT.Exp).then_inc(s["e"], 1)

        @block.vector
        def _(dve):
            for k in ("x2", "x3", "alo", "nlo", "qc", "rt", "pos", "mwl"):
                dve.sem_inc(s[k], CR)
            dve.sem_inc(s["st30"], 16)
            dve.sem_inc(s["st31"], 16)
            for i in range(3):
                o = slice(i * WPIECE, (i + 1) * WPIECE)
                dve.wait_ge(s["wh"], i + 1)
                dve.tensor_tensor(ww[:, 1, o], wraw[i], ww[:, 0, o].bitcast(F32),
                                  ALU.subtract).then_inc(s["wl"], 1)
            dve.wait_ge(s["pool"], 11)
            dve.wait_ge(s["c"], 16 * 7)
            def att_low(r, j):
                dve.wait_ge(s["ahi"], r * QT + j + 1 + CR)
                dve.tensor_tensor(ap[:, j % 2, 1, :, :], att[:, j % 2, :, :],
                                  ap[:, j % 2, 0, :, :].bitcast(F32), ALU.subtract).then_inc(s["alo"], 1)

            def norm(r, i, k, src, dst, sem):
                c = lnorm(r, i, k)
                dve.bn_stats(st[:, k, :], src).then_inc(s["bn"], 1)
                wait_alone(dve, s["bn"], c, s["any"])
                dve.bn_aggr(mv[:, k, :], st[:, k, :]).then_inc(s["mv"], 1)
                dve.wait_ge(s["sd"], c)
                dve.reciprocal(rs[:, k:k + 1], sd[:, k:k + 1]).then_inc(s["rs"], 1)
                dve.wait_ge(s["rs"], c)
                dve.tensor_scalar(dst, src, mv[:, k, 0:1], rs[:, k:k + 1], ALU.subtract,
                                  ALU.mult).then_inc(s[sem], 1)

            def step(r, i):
                if here(r, i - 1):
                    j = i - 1
                    dve.wait_ge(s["nhi"], r * QT + j + 1)
                    dve.tensor_tensor(nT[:, j % 2, 1, :, :],
                                      pT[slot("n", r, j)][:, :].rearrange("p (e t) -> p e t", e=ET),
                                      nT[:, j % 2, 0, :, :].bitcast(F32), ALU.subtract).then_inc(s["nlo"], 1)
                if here(r, i - 2):
                    j = i - 2
                    dve.wait_ge(s["qhi"], r * QT + j + 1)
                    dve.tensor_tensor(qT[:, j % 2, 1, :, :], qf[:, :].rearrange("p (e t) -> p e t", e=ET),
                                      qT[:, j % 2, 0, :, :].bitcast(F32), ALU.subtract).then_inc(s["qlo"], 1)
                if here(r, i + 1):
                    att_low(r, i + 1)
                if here(r, i):
                    dve.wait_ge(s["A"], r * QT + i + 1)
                    dve.wait_ge(s[f"xl{i % 2}"], 16 * (r * QT // 2 + i // 2 + 1))
                    if after(r, i, 2):
                        dve.wait_ge(s["x2b"], r * QT + i - 1)
                    dve.tensor_tensor(x2[:, i % 2, :], pA[i % 2][:, :], x[:, i % 2, :],
                                      ALU.add).then_inc(s["x2"], 1)
                    dve.wait_ge(s["x2"], r * QT + i + 1 + CR)
                    norm(r, i, 0, x2[:, i % 2, :], n2[:, i % 2, :], "n2")
                b = memory_of(r, i)
                if b is not None:
                    for q in range(4):
                        dve.wait_ge(s["mwh"], 4 * b + q + 1)
                        dve.tensor_tensor(mw[:, 1, q, :], product_bank(i, q)[:, :], mw[:, 0, q, :].bitcast(F32),
                                          ALU.subtract).then_inc(s["mwl"], 1)
                if here(r, i - 1):
                    j = i - 1
                    c = r * QT + j + 1
                    q3 = pQ[:, :].rearrange("p (h j) -> p h j", h=XH)
                    dve.wait_ge(s["Q"], c)
                    dve.tensor_reduce(hs1[:, j % 2, :], q3, AXX, ALU.add).then_inc(s["hvar"], 1)
                    dve.wait_ge(s["hvar"], 2 * c - 1)
                    if after(r, j, 2):
                        dve.wait_ge(s["qn"], c - 2)
                    dve.tensor_scalar(hs3[:, j % 2, :], hs1[:, j % 2, :], 1.0 / XD, None,
                                      ALU.mult).then_inc(s["hmean"], 1)
                    dve.wait_ge(s["hmean"], c)
                    dve.tensor_tensor(qc[:, j % 2, :].rearrange("p (h j) -> p h j", h=XH), q3,
                                      hs3[:, j % 2, :].unsqueeze(2).broadcast_to([P, XH, XD]),
                                      ALU.subtract).then_inc(s["qc"], 1)
                    dve.wait_ge(s["sq"], c)
                    dve.tensor_reduce(hs1[:, j % 2, :], sq[:, :].rearrange("p (h j) -> p h j", h=XH), AXX,
                                      ALU.add).then_inc(s["hvar"], 1)
                    dve.wait_ge(s["hsd"], c)
                    dve.reciprocal(hs3[:, j % 2, :], hs2[:, j % 2, :]).then_inc(s["hrs"], 1)
                if here(r, i - 2):
                    j = i - 2
                    c = r * QT + j + 1
                    dve.wait_ge(s["M"], c)
                    dve.wait_ge(s["x2b"], c)
                    dve.wait_ge(s[f"st3{j % 2}"], 16 * (r * QT // 2 + j // 2 + 1))
                    dve.tensor_tensor(x3[:, j % 2, :], pM[:, :], x2b[:, j % 4, :], ALU.add).then_inc(s["x3"], 1)
                    dve.wait_ge(s["x3"], c + CR)
                    dve.wait_ge(s["scd"], c)
                    norm(r, i, 1, x3[:, j % 2, :], hn[:, j % QT, :], "hn")
                if i == LAG + QT - 1:
                    wait_alone(dve, s["dc"], 4 * QT * (r + 1), s["any"])
                    dve.tensor_copy(route["top"][:, bass.ds(r * QT, QT), :], top8[:, :, 0:2]).then_inc(s["keep"], 1)
                    dve.wait_ge(s["keep"], 2 * r + 1)
                if here(r, i - 3):
                    j = i - 3
                    c = r * QT + j + 1
                    dve.wait_ge(s["R"], c)
                    dve.tensor_tensor(lg[:, :], pR[:, 0:NE], rbias[:, :], ALU.add).then_inc(s["rt"], 1)
                    wait_alone(dve, s["rt"], c + CR, s["any"])
                    u = (r * QT + j) * 4
                    dve.max(top8[:, j % QT, :], lg[:, :]).then_inc(s["dc"], 1)
                    wait_alone(dve, s["dc"], u + 1, s["any"])
                    dve.max_index(ix8[:, :], top8[:, j % QT, :], lg[:, :]).then_inc(s["dc"], 1)
                    dve.wait_ge(s["dc"], u + 2)
                    dve.tensor_copy(idx[:, j % 2, :], ix8[:, :]).then_inc(s["dc"], 1)
                    dve.wait_ge(s["dc"], u + 3)
                    dve.tensor_scalar(m1[:, :], iota8[:, :], idx[:, j % 2, 0:1], None,
                                      ALU.is_equal).then_inc(s["dc"], 1)
                    dve.wait_ge(s["dc"], u + 4)
                    dve.scalar_tensor_tensor(out=msum[:, j % 2, :], in0=iota8[:, :], scalar=idx[:, j % 2, 1:2],
                                             in1=m1[:, :], op0=ALU.is_equal, op1=ALU.add
                                             ).then_inc(s["ms"], 1)
                if here(r, i - 4):
                    j = i - 4
                    c = r * QT + j + 1
                    u = (r * QT + j) * 4
                    dve.wait_ge(s["rank"], c)
                    dve.tensor_tensor(pr[:, :], pW[:, 0:NE], base[:, :], ALU.add).then_inc(s["cnt"], 1)
                    dve.tensor_tensor(cum[:, :], cum[:, :], msum[:, j % 2, :], ALU.add).then_inc(s["cumd"], 1)
                    dve.wait_ge(s["cnt"], u + 1)
                    for k in range(2):
                        if k:
                            dve.wait_ge(s["cnt"], u + 2)
                        dve.scalar_tensor_tensor(out=junk[:, :], in0=iota8[:, :], scalar=idx[:, j % 2, k:k + 1],
                                                 in1=pr[:, :], op0=ALU.is_equal, op1=ALU.mult,
                                                 accum_out=pf[:, j % 2, k:k + 1]).then_inc(s["cnt"], 1)
                    dve.wait_ge(s["cnt"], u + 3)
                    dve.wait_ge(s["cumd"], c)
                    dve.tensor_copy(pi[:, j % QT, :], pf[:, j % 2, :]).then_inc(s["pos"], 1)
                    dve.sem_inc(s["cnt"], 1)
                if i == LAG + QT - 1:
                    wait_alone(dve, s["pos"], (r + 1) * QT + CR, s["any"])
                    dve.tensor_copy(route["pos"][:, bass.ds(r * QT, QT), :], pi[:, :, :]).then_inc(s["keep"], 1)
                    dve.wait_ge(s["keep"], 2 * r + 2)

            att_low(0, 0)
            sweep(dve, step)
            ch = Chain(dve, s["tb"])
            dve.tensor_tensor(e2[:, :], route["top"][:, :, 1], route["top"][:, :, 0], ALU.subtract).then_inc(s["e"], 1)
            dve.wait_ge(s["e"], 2)
            ch.step(dve.tensor_scalar(route["w"][:, :, 0], e2[:, :], 1.0, None, ALU.add))
            ch.step(dve.reciprocal(route["w"][:, :, 0], route["w"][:, :, 0]))
            ch.step(dve.tensor_tensor(route["w"][:, :, 1], e2[:, :], route["w"][:, :, 0], ALU.mult))
            dve.wait_ge(s["tot"], 1)
            ch.step(dve.tensor_copy(cnt[:, :], pW[:, 0:NE]))
            ch.step(dve.tensor_scalar(nb[:, :], cnt[:, :], 0.0, None, ALU.is_gt))
            for m in range(1, TOK // BLK):
                ch.step(dve.scalar_tensor_tensor(out=nb[:, :], in0=cnt[:, :], scalar=float(m * BLK), in1=nb[:, :],
                                                 op0=ALU.is_gt, op1=ALU.add))
            ch.step(dve.tensor_copy(end[:, 0:1], nb[:, 0:1]))
            for e in range(1, NE):
                ch.step(dve.tensor_tensor(end[:, e:e + 1], end[:, e - 1:e], nb[:, e:e + 1], ALU.add))
            E, before, t0, t1 = (tb[:, k, :] for k in range(4))
            ch.do(dve.memset(tb[:, 0:2, :], 0.0))
            ch.sync()
            for e in range(NE):
                ch.step(dve.tensor_scalar(t0, itf[:, :], end[:, e:e + 1], None, ALU.is_ge))
                ch.step(dve.tensor_tensor(E, E, t0, ALU.add))
                ch.step(dve.scalar_tensor_tensor(out=before, in0=t0, scalar=nb[:, e:e + 1], in1=before,
                                                 op0=ALU.mult, op1=ALU.add))
            ch.step(dve.tensor_tensor(before, itf[:, :], before, ALU.subtract))
            ch.step(dve.tensor_scalar(before, before, float(BLK), None, ALU.mult))
            ch.step(dve.tensor_scalar(t1, E, NE - 0.5, None, ALU.is_lt))
            ch.step(dve.tensor_tensor(before, before, t1, ALU.mult))
            ch.step(dve.tensor_scalar(E, E, NE - 1.0, None, ALU.min))
            ch.step(dve.tensor_copy(route["tab"][:, 0, :], E))
            ch.step(dve.scalar_tensor_tensor(out=t0, in0=E, scalar=float(REG), in1=before,
                                             op0=ALU.mult, op1=ALU.add))
            ch.step(dve.tensor_copy(route["tab"][:, 1, :], t0))
            ch.step(dve.tensor_tensor(nb[:, :], end[:, :], nb[:, :], ALU.subtract))
            ch.step(dve.scalar_tensor_tensor(out=nb[:, :], in0=nb[:, :], scalar=float(BLK), in1=base[:, :],
                                             op0=ALU.mult, op1=ALU.subtract))
            posf, yrow, mask = (tp[:, k, :] for k in range(3))
            ch.step(dve.tensor_copy(posf, route["pos"][:, :, :].rearrange("p t k -> p (t k)")))
            ch.step(dve.tensor_copy(yrow, posf))
            for e in range(NE):
                ch.step(dve.tensor_scalar(mask, posf, float(e * REG), None, ALU.is_ge))
                ch.step(dve.scalar_tensor_tensor(out=mask, in0=posf, scalar=float((e + 1) * REG), in1=mask,
                                                 op0=ALU.is_lt, op1=ALU.mult))
                ch.step(dve.scalar_tensor_tensor(out=yrow, in0=mask, scalar=nb[:, e:e + 1], in1=yrow,
                                                 op0=ALU.mult, op1=ALU.add))
            ch.step(dve.tensor_copy(route["pos"][:, :, :].rearrange("p t k -> p (t k)"), yrow))
            ch.step(dve.tensor_tensor(cnt[:, :], cnt[:, :], base[:, :], ALU.add))
            dve.tensor_copy(route["tab"][:, 3, 0:NE], cnt[:, :]).then_inc(s["fin"], 1)


def expert_phase(nc, io, dram, route):
    with Room(nc, "e_") as rm:
        WM = ET * D
        RT = BLK // P
        raw = rm.sb("raw", [P, 3, WM])
        w = rm.sb("w", [P, 3, 2, WM], F32R)
        rows = rm.sb("rows", [P, RT, D])
        hT = rm.sb("hT", [P, 2, ET, BLK], F32R)
        sil = rm.sb("sil", [P, 2, BLK])
        a32 = rm.sb("a32", [P, 2, BLK])
        aT = rm.sb("aT", [P, 2, ET, BLK], F32R)
        y = rm.sb("y", [P, RT, D])
        ident = rm.sb("ident", [P, P])
        pT, pG, pU, pY = ([rm.ps(f"{n}{i}", [P, 512]) for i in range(2)] for n in "TGUY")
        names = "any id rows rawg rawu rawd whi wlo T thi tlo G U sil mul ahi alo Y y st".split()
        s = {k: rm.sem(k) for k in names}
        block = rm.ctx.enter_context(nc.Block())

        @block.sync
        def _(sp):
            def entry(kind, j, top):
                return sp.value_load(route["tab"][0:1, kind, bass.ds(j, 1)], min_val=0, max_val=top)

            def load_rows(j):
                r = entry(1, j, NE * REG - BLK)
                sp.dma_start(rows[:, :, :], dram["hs"][bass.ds(r, BLK), :].rearrange("(t p) d -> p t d", p=P)
                             ).then_inc(s["rows"], 16)

            def load_weight(k, e):
                sp.dma_start(raw[:, k, :], io["we"][bass.ds(e, 1), k].rearrange("o p n -> (o p) n")
                             ).then_inc(s[("rawg", "rawu", "rawd")[k]], 16)

            sp.dma_start(ident[:, :], io["ident"]).then_inc(s["id"], 16)
            load_rows(0)
            e0 = entry(0, 0, NE - 1)
            for k in range(3):
                load_weight(k, e0)
            with sp.Fori(0, NBLK) as j:
                e = entry(0, j + 1, NE - 1)
                wait_alone(sp, s["tlo"], 4 * j + 4 + 2, s["any"])
                load_rows(j + 1)
                for k in range(2):
                    wait_alone(sp, s["wlo"], 3 * j + k + 1, s["any"])
                    load_weight(k, e)
                wait_alone(sp, s["wlo"], 3 * j + 3, s["any"])
                load_weight(2, e)
                wait_alone(sp, s["y"], 4 * j + 4 + 2, s["any"])
                sp.dma_start(dram["ys"][bass.ds(j * BLK, BLK), :].rearrange("(t p) d -> p t d", p=P),
                             y[:, :, :]).then_inc(s["st"], 16)
            for k in ("rows", "rawg", "rawu", "rawd", "st"):
                sp.wait_ge(s[k], 16 * (NBLK + 1))

        def split(eng, j, k, part):
            if part == 0:
                eng.wait_ge(s[("rawg", "rawu", "rawd")[k]], 16 * (j + 1))
                eng.activation(w[:, k, 0, :], raw[:, k, :], ACT.Copy).then_inc(s["whi"], 1)
            else:
                eng.wait_ge(s["whi"], 3 * j + k + 1)
                eng.tensor_tensor(w[:, k, 1, :], raw[:, k, :], w[:, k, 0, :].bitcast(F32),
                                  ALU.subtract).then_inc(s["wlo"], 1)

        @block.tensor
        def _(pe):
            def parts(out, lhs, rhs, k):
                pe.matmul(out, lhs(0), rhs(0), start=k == 0, stop=False)
                pe.matmul(out, lhs(0), rhs(1), start=False, stop=False)
                return pe.matmul(out, lhs(1), rhs(0), start=False, stop=k == ET - 1)

            def turn(j, e):
                pe.wait_ge(s["rows"], 16 * (j + 1))
                pe.wait_ge(s["tlo"], 4 * j + e - 1 + 2)
                for t in range(RT):
                    mm = pe.transpose(pT[e % 2][:, t * P:(t + 1) * P], rows[:, t, e * P:(e + 1) * P],
                                      ident[:, :])
                mm.then_inc(s["T"], 1)

            def down(t, f0, f1):
                for f in range(f0, f1):
                    mm = parts(pY[t % 2][:, :], lambda a: aT[:, a, f, t * P:(t + 1) * P],
                               lambda a: w[:, 2, a, f * D:(f + 1) * D], f)
                return mm

            pe.wait_ge(s["id"], 16)
            for e in range(ET):
                turn(0, e)
            with pe.Fori(0, NBLK) as j:
                pe.wait_ge(s["tlo"], 4 * j + 4 + 2)
                for f in range(ET):
                    pe.wait_ge(s["mul"], 4 * j + f - 1 + 2)
                    for k, out, sem in ((0, pG, "G"), (1, pU, "U")):
                        if f == 0:
                            pe.wait_ge(s["wlo"], 3 * j + k + 1)
                        for e in range(ET):
                            mm = parts(out[f % 2][:, :],
                                       lambda a: w[:, k, a, e * D + f * P:e * D + (f + 1) * P],
                                       lambda a: hT[:, a, e, :], e)
                        mm.then_inc(s[sem], 1)
                    if f in (1, 2):
                        turn(j + 1, f - 1)
                pe.wait_ge(s["alo"], 4 * j + 3)
                pe.wait_ge(s["wlo"], 3 * j + 3)
                for t in range(2):
                    pe.wait_ge(s["y"], 4 * j + t - 1 + 2)
                    down(t, 0, ET - 1)
                pe.wait_ge(s["alo"], 4 * j + 4)
                for t in range(2):
                    down(t, ET - 1, ET).then_inc(s["Y"], 1)
                for t in range(2, RT):
                    turn(j + 1, t)
                    pe.wait_ge(s["y"], 4 * j + t - 1 + 2)
                    down(t, 0, ET).then_inc(s["Y"], 1)

        @block.scalar
        def _(act):
            act.sem_inc(s["y"], 2)

            def turn_high(j, e):
                act.wait_ge(s["T"], 4 * j + e + 1)
                act.activation(hT[:, 0, e, :], pT[e % 2][:, :], ACT.Copy).then_inc(s["thi"], 1)

            def row_out(j, t):
                act.wait_ge(s["Y"], 4 * j + t + 1 + 1)
                act.activation(y[:, t, :], pY[t % 2][:, :], ACT.Copy).then_inc(s["y"], 1)

            for e in range(ET):
                turn_high(0, e)
            split(act, 0, 0, 0)
            split(act, 0, 1, 0)
            with act.Fori(0, NBLK) as j:
                for f in range(ET):
                    act.wait_ge(s["G"], 4 * j + f + 1)
                    act.wait_ge(s["mul"], 4 * j + f - 1 + 2)
                    act.activation(sil[:, f % 2, :], pG[f % 2][:, :], ACT.Silu).then_inc(s["sil"], 1)
                    act.wait_ge(s["mul"], 4 * j + f + 1 + 2)
                    act.activation(aT[:, 0, f, :], a32[:, f % 2, :], ACT.Copy).then_inc(s["ahi"], 1)
                    if f == 1:
                        act.wait_ge(s["Y"], 4 * j + 1)
                        split(act, j, 2, 0)
                act.wait_ge(s["U"], 4 * j + 4)
                turn_high(j + 1, 0)
                turn_high(j + 1, 1)
                split(act, j + 1, 0, 0)
                act.wait_ge(s["st"], 16 * j + 16)
                for t in range(2):
                    row_out(j, t)
                    turn_high(j + 1, t + 2)
                split(act, j + 1, 1, 0)
                for t in range(2, RT):
                    row_out(j, t)

        @block.vector
        def _(dve):
            dve.sem_inc(s["tlo"], 2)
            dve.sem_inc(s["mul"], 2)
            dve.sem_inc(s["st"], 16)
            dve.sem_inc(s["Y"], 1)

            def turn_low(j, e):
                dve.wait_ge(s["thi"], 4 * j + e + 1)
                dve.tensor_tensor(hT[:, 1, e, :], pT[e % 2][:, :], hT[:, 0, e, :].bitcast(F32),
                                  ALU.subtract).then_inc(s["tlo"], 1)

            for e in range(ET):
                turn_low(0, e)
            split(dve, 0, 0, 1)
            split(dve, 0, 1, 1)
            with dve.Fori(0, NBLK) as j:
                for f in range(ET):
                    dve.wait_ge(s["U"], 4 * j + f + 1)
                    dve.wait_ge(s["sil"], 4 * j + f + 1)
                    dve.tensor_tensor(a32[:, f % 2, :], pU[f % 2][:, :], sil[:, f % 2, :],
                                      ALU.mult).then_inc(s["mul"], 1)
                    dve.wait_ge(s["ahi"], 4 * j + f + 1)
                    dve.tensor_tensor(aT[:, 1, f, :], a32[:, f % 2, :], aT[:, 0, f, :].bitcast(F32),
                                      ALU.subtract).then_inc(s["alo"], 1)
                    if f == 1:
                        split(dve, j, 2, 1)
                for e in range(2):
                    turn_low(j + 1, e)
                split(dve, j + 1, 0, 1)
                for e in range(2, ET):
                    turn_low(j + 1, e)
                split(dve, j + 1, 1, 1)


def combine_phase(nc, io, dram, route):
    R = 4
    with Room(nc, "o_") as rm:
        x = rm.sb("x", [P, R, D])
        y = rm.sb("y", [P, R, 2, D])
        o = rm.sb("o", [P, R, D])
        pi = rm.sb("pi", [P, R, 2], I32)
        w = rm.sb("w", [P, R, 2])
        s_x, s_y, s_o = ([rm.sem(f"{n}{i}") for i in range(R)] for n in "xyo")
        s_any = rm.sem("any")
        s_pi = rm.sem("pi")
        s_w = rm.sem("w")
        s_add = rm.sem("add")
        block = rm.ctx.enter_context(nc.Block())
        N = NT // R

        @block.sync
        def _(sp):
            with sp.Fori(0, N) as i:
                for k in range(R):
                    wait_alone(sp, s_add, 2 * (i * R + k) + 2, s_any)
                    sp.dma_start(x[:, k, :], dram["x3"][bass.ds((i * R + k) * P, P), :]).then_inc(s_x[k], 16)
            for k in range(R):
                sp.wait_ge(s_x[k], 16 * N)

        @block.gpsimd
        def _(gp):
            with gp.Fori(0, N) as i:
                for k in range(R):
                    wait_alone(gp, s_pi, i * R + k + 1, s_any)
                    wait_alone(gp, s_add, 2 * (i * R + k) + 2, s_any)
                    for a in range(2):
                        gp.indirect_dma_start(y[:, k, a, :], None, dram["ys"][:, :],
                                              bass.IndirectOffsetOnAxis(ap=pi[:, k, a:a + 1], axis=0)
                                              ).then_inc(s_y[k], 16)
            for k in range(R):
                gp.wait_ge(s_y[k], 32 * N)

        @block.vector
        def _(dve):
            dve.sem_inc(s_add, 2 * R)
            for k in range(R):
                dve.sem_inc(s_o[k], 16)
            with dve.Fori(0, N) as i:
                for k in range(R):
                    t = i * R + k
                    wait_alone(dve, s_add, 2 * t + 2, s_any)
                    dve.tensor_copy(pi[:, k, :].unsqueeze(1), route["pos"][:, bass.ds(t, 1), :]).then_inc(s_pi, 1)
                    dve.tensor_copy(w[:, k, :].unsqueeze(1), route["w"][:, bass.ds(t, 1), :]).then_inc(s_w, 1)
                for k in range(R):
                    t = i * R + k
                    dve.wait_ge(s_w, t + 1)
                    dve.wait_ge(s_x[k], 16 * i + 16)
                    dve.wait_ge(s_y[k], 32 * i + 32)
                    dve.wait_ge(s_o[k], 16 * i + 16)
                    dve.scalar_tensor_tensor(out=x[:, k, :], in0=y[:, k, 0, :], scalar=w[:, k, 0:1],
                                             in1=x[:, k, :], op0=ALU.mult, op1=ALU.add).then_inc(s_add, 1)
                    dve.wait_ge(s_add, 2 * t + 1 + 2 * R)
                    dve.scalar_tensor_tensor(out=o[:, k, :], in0=y[:, k, 1, :], scalar=w[:, k, 1:2],
                                             in1=x[:, k, :], op0=ALU.mult, op1=ALU.add).then_inc(s_add, 1)

        @block.scalar
        def _(act):
            with act.Fori(0, N) as i:
                for k in range(R):
                    t = i * R + k
                    wait_alone(act, s_add, 2 * t + 2 + 2 * R, s_any)
                    act.dma_start(io["out"][bass.ds(t * P, P), :], o[:, k, :]).then_inc(s_o[k], 16)
            for k in range(R):
                act.wait_ge(s_o[k], 16 * N + 16)


def kernel(**inputs):
    import concourse.bacc as bacc
    from concourse.bass_utils import run_bass_kernel_spmd as run

    def rows(w):
        return w.reshape(-1, P, w.shape[1]).transpose(1, 0, 2).reshape(P, -1)

    a = {k: np.ascontiguousarray(v) for k, v in inputs.items()}
    q, k, v = np.split(a["L0_attn_W_qkv"], 3, axis=1)

    def halves(w, g):
        w = w.reshape(D, H, HD // 2, 2)[:, g * GH:(g + 1) * GH]
        return w.transpose(0, 3, 1, 2).reshape(D, 2 * P)

    wts = [rows(np.concatenate([halves(q, g), halves(k, g), v[:, g * GH * HD:(g + 1) * GH * HD]], axis=1))
           for g in range(G)]
    tail = np.concatenate([rows(a["L0_attn_W_out"]), rows(a["L0_xattn_Wq"].T)], axis=1)
    wts += [tail[:, :WCOLS], tail[:, WCOLS:]]
    freqs = 1.0 / np.float32(10000.0) ** (np.arange(0, HD, 2, dtype=np.float32) / np.float32(HD))
    angles = (np.arange(T, dtype=np.float32)[:, None] * freqs.astype(np.float32)[None, :]).astype(np.float32)
    rot = np.tile(angles.T, (GH, 1))
    arrays = {
        "x": a["x"].reshape(TOK, D), "ctx": a["ctx_1024"].reshape(B * TC, D), "wts": np.stack(wts),
        "wkT": a["L0_xattn_Wk"].T, "wvT": a["L0_xattn_Wv"].T,
        "wgT": np.concatenate([a["L0_xattn_Wbeta"], a["L0_xattn_Walpha"]], axis=0).T,
        "gbias": np.concatenate([a["L0_xattn_bbeta"], a["L0_xattn_balpha"]]),
        "gk": a["L0_xattn_gk"], "bk": a["L0_xattn_bk"],
        "woT": a["L0_xattn_Wo"].T, "bo": a["L0_xattn_bo"],
        "gq": np.tile(a["L0_xattn_gq"], P // XD)[:, None], "bq": np.tile(a["L0_xattn_bq"], P // XD)[:, None],
        "rw": a["L0_ffn_router_w"], "rb": a["L0_ffn_router_b"],
        "we": np.stack([np.stack([rows(a[n][e]) for n in ("L0_ffn_we_gate", "L0_ffn_we_up", "L0_ffn_we_down")])
                        for e in range(NE)]),
        "cos": np.cos(rot), "sin": np.sin(rot), "ident": np.eye(P, dtype=np.float32),
    }
    arrays = {"in_" + n: np.ascontiguousarray(x) for n, x in arrays.items()}
    nc = bacc.Bacc("TRN2", target_bir_lowering=False, num_devices=1)
    io = {n[3:]: nc.dram_tensor(n, x.shape, mybir.dt.from_np(x.dtype), kind="ExternalInput").ap()
          for n, x in arrays.items()}
    io["out"] = nc.dram_tensor("out", (TOK, D), F32, kind="ExternalOutput").ap()
    program(nc, io)
    r = run(nc, [arrays], core_ids=[0])
    return r.results[0]["out"].reshape(B, T, D)
```
